# Optimizing a Trainium2 kernel written in Bass

```python
import numpy as np
import jax
import jax.numpy as jnp

def _softmax(x, axis=-1):
    return jax.nn.softmax(x, axis=axis)

def _gelu(x):
    return jax.nn.gelu(x, approximate=True)

def _silu(x):
    return jax.nn.silu(x)

def _sigmoid(x):
    return jax.nn.sigmoid(x)

def _layernorm(x, axis=-1, eps=1e-05):
    m = jnp.mean(x, axis=axis, keepdims=True)
    v = jnp.var(x, axis=axis, keepdims=True)
    return (x - m) / jnp.sqrt(v + eps)

def _scatter_add(tgt, idx, src, axis=0):
    return tgt.at[idx].add(src)

def _segment_sum(src, seg, n):
    return jax.ops.segment_sum(src, seg, n)
kernel_name = 'mk_xattn_ffn_d1_seqx_r8_830582'

def setup_inputs(seed: int=0):
    np.random.seed(seed)
    _w = jnp.asarray

    def _rec_inputs():
        import jax
        import jax.numpy as jnp
        _rk = jax.random.key(seed)
        x = -0.0002928 + 1 * jax.random.normal(jax.random.fold_in(_rk, 1), (128, 64, 128), jnp.float32)
        _lenS = 64 - jax.random.randint(jax.random.fold_in(_rk, 7), (128,), 0, max(1, 64 // 4) + 1, jnp.int32)
        _lenS2 = 64 - jax.random.randint(jax.random.fold_in(_rk, 8), (128,), 0, max(1, 64 // 4) + 1, jnp.int32)
        _ctx_1024P = jax.random.normal(jax.random.fold_in(_rk, 11), (128, 16, 128), jnp.float32)
        _ctx_1024c = jax.random.dirichlet(jax.random.fold_in(_rk, 511), 0.3 * jnp.ones((16,), jnp.float32), (128, 64))
        _ctx_1024t = jnp.einsum('bsk,bkd->bsd', _ctx_1024c, _ctx_1024P)
        _ctx_1024t = _ctx_1024t * jax.lax.rsqrt(jnp.mean(jnp.square(_ctx_1024t)) + 1e-12) * 0.953939
        ctx_1024 = -1.39393e-06 + 0.999914 * (_ctx_1024t + 0.3 * jax.random.normal(jax.random.fold_in(_rk, 611), (128, 64, 128), jnp.float32))
        return (x, ctx_1024)
    x, ctx_1024 = _rec_inputs()

    def _L0_xattn_setup():
        import jax, jax.numpy as jnp
        import numpy as np
        D_K = 128
        H = 16
        D_H = D_K // H
        key = jax.random.key(seed)
        ks = jax.random.split(key, 11)
        B, S = (2, 256)
        scale = 1.0 / np.sqrt(D_K)
        inp = {'Q': jax.random.normal(ks[0], (B, S, D_K), jnp.float32), 'K': jax.random.normal(ks[1], (B, S, D_K), jnp.float32), 'V': jax.random.normal(ks[2], (B, S, D_K), jnp.float32), 'Wq': jax.random.normal(ks[3], (D_K, D_K), jnp.float32) * scale, 'bq': jax.random.normal(ks[4], (D_K,), jnp.float32) * 0.01, 'Wk': jax.random.normal(ks[5], (D_K, D_K), jnp.float32) * scale, 'bk': jax.random.normal(ks[6], (D_K,), jnp.float32) * 0.01, 'Wv': jax.random.normal(ks[7], (D_K, D_K), jnp.float32) * scale, 'bv': jax.random.normal(ks[8], (D_K,), jnp.float32) * 0.01, 'Wo': jax.random.normal(ks[9], (D_K, D_K), jnp.float32) * scale, 'bo': jax.random.normal(ks[10], (D_K,), jnp.float32) * 0.01}
        return inp
    _L0_xattn_all = _L0_xattn_setup()
    _L0_xattn_in = {k: v for k, v in _L0_xattn_all.items() if k in ('Wq', 'bq', 'Wk', 'bk', 'Wv', 'bv', 'Wo', 'bo')}
    del _L0_xattn_all

    def _L0_ffn_setup():
        import jax, jax.numpy as jnp
        import numpy as np
        B, L, C1, C2, K, K_IN = (4, 128, 128, 128, 32, 32)
        BN_EPS = 1e-05

        def _gated_bottleneck(x2d, conv_w, conv_b, gamma, beta, lin_w, lin_b):
            n = x2d.shape[0]
            g = conv_w.shape[0]
            xc = jnp.einsum('ngf,gf->ng', x2d.reshape(n, g, 4), conv_w) + conv_b
            mean = jnp.mean(xc, axis=0)
            var = jnp.mean((xc - mean) ** 2, axis=0)
            xn = (xc - mean) * jax.lax.rsqrt(var + BN_EPS) * gamma + beta
            xa = jax.nn.gelu(xn, approximate=False)
            return xa @ lin_w.T + lin_b
        key = jax.random.key(seed)
        ks = jax.random.split(key, 8)
        g = C1 // 4
        w_std = (2.0 / C2) ** 0.5
        lin_std = (1.0 / g) ** 0.5
        return {'x': jax.random.normal(ks[0], (B, L, C1), jnp.float32), 'weight': jax.random.normal(ks[1], (C1, C2), jnp.float32) * w_std, 'bias': jnp.zeros((C2,), jnp.float32), 'so_conv_w': jax.random.normal(ks[2], (g, 4), jnp.float32) * 0.5, 'so_conv_b': jnp.zeros((g,), jnp.float32), 'so_gamma': jnp.ones((g,), jnp.float32), 'so_beta': jnp.zeros((g,), jnp.float32), 'so_lin_w': jax.random.normal(ks[3], (C2, g), jnp.float32) * lin_std, 'so_lin_b': jnp.zeros((C2,), jnp.float32), 'si_conv_w': jax.random.normal(ks[4], (g, 4), jnp.float32) * 0.5, 'si_conv_b': jnp.zeros((g,), jnp.float32), 'si_gamma': jnp.ones((g,), jnp.float32), 'si_beta': jnp.zeros((g,), jnp.float32), 'si_lin_w': jax.random.normal(ks[5], (C1, g), jnp.float32) * lin_std, 'si_lin_b': jnp.zeros((C1,), jnp.float32)}
    _L0_ffn_all = _L0_ffn_setup()
    _L0_ffn_in = {k: v for k, v in _L0_ffn_all.items() if k in ('weight', 'bias', 'so_conv_w', 'so_conv_b', 'so_gamma', 'so_beta', 'so_lin_w', 'so_lin_b', 'si_conv_w', 'si_conv_b', 'si_gamma', 'si_beta', 'si_lin_w', 'si_lin_b')}
    del _L0_ffn_all
    return {'x': x, 'ctx_1024': ctx_1024, 'L0_xattn_Wq': _L0_xattn_in['Wq'], 'L0_xattn_bq': _L0_xattn_in['bq'], 'L0_xattn_Wk': _L0_xattn_in['Wk'], 'L0_xattn_bk': _L0_xattn_in['bk'], 'L0_xattn_Wv': _L0_xattn_in['Wv'], 'L0_xattn_bv': _L0_xattn_in['bv'], 'L0_xattn_Wo': _L0_xattn_in['Wo'], 'L0_xattn_bo': _L0_xattn_in['bo'], 'L0_ffn_weight': _L0_ffn_in['weight'], 'L0_ffn_bias': _L0_ffn_in['bias'], 'L0_ffn_so_conv_w': _L0_ffn_in['so_conv_w'], 'L0_ffn_so_conv_b': _L0_ffn_in['so_conv_b'], 'L0_ffn_so_gamma': _L0_ffn_in['so_gamma'], 'L0_ffn_so_beta': _L0_ffn_in['so_beta'], 'L0_ffn_so_lin_w': _L0_ffn_in['so_lin_w'], 'L0_ffn_so_lin_b': _L0_ffn_in['so_lin_b'], 'L0_ffn_si_conv_w': _L0_ffn_in['si_conv_w'], 'L0_ffn_si_conv_b': _L0_ffn_in['si_conv_b'], 'L0_ffn_si_gamma': _L0_ffn_in['si_gamma'], 'L0_ffn_si_beta': _L0_ffn_in['si_beta'], 'L0_ffn_si_lin_w': _L0_ffn_in['si_lin_w'], 'L0_ffn_si_lin_b': _L0_ffn_in['si_lin_b']}

def reference(x, ctx_1024, L0_xattn_Wq, L0_xattn_bq, L0_xattn_Wk, L0_xattn_bk, L0_xattn_Wv, L0_xattn_bv, L0_xattn_Wo, L0_xattn_bo, L0_ffn_weight, L0_ffn_bias, L0_ffn_so_conv_w, L0_ffn_so_conv_b, L0_ffn_so_gamma, L0_ffn_so_beta, L0_ffn_so_lin_w, L0_ffn_so_lin_b, L0_ffn_si_conv_w, L0_ffn_si_conv_b, L0_ffn_si_gamma, L0_ffn_si_beta, L0_ffn_si_lin_w, L0_ffn_si_lin_b):
    import jax
    import jax.numpy as jnp

    def _L0_xattn_ref(Q, K, V, Wq, bq, Wk, bk, Wv, bv, Wo, bo):
        import jax, jax.numpy as jnp
        import numpy as np
        D_K = 128
        H = 16
        D_H = D_K // H
        B, S, _ = Q.shape
        inv_sqrt_dh = 1.0 / np.sqrt(D_H).astype(np.float32)
        q = (Q @ Wq.T + bq).reshape(B, S, H, D_H).transpose(0, 2, 1, 3)
        k = (K @ Wk.T + bk).reshape(B, S, H, D_H).transpose(0, 2, 1, 3)
        v = (V @ Wv.T + bv).reshape(B, S, H, D_H).transpose(0, 2, 1, 3)
        scores = jnp.einsum('bhqd,bhkd->bhqk', q, k) * inv_sqrt_dh
        attn = jax.nn.softmax(scores, axis=-1)
        ctx = jnp.einsum('bhqk,bhkd->bhqd', attn, v)
        ctx = ctx.transpose(0, 2, 1, 3).reshape(B, S, D_K)
        return ctx @ Wo.T + bo

    def _L0_ffn_ref(x, weight, bias, so_conv_w, so_conv_b, so_gamma, so_beta, so_lin_w, so_lin_b, si_conv_w, si_conv_b, si_gamma, si_beta, si_lin_w, si_lin_b):
        import jax, jax.numpy as jnp
        import numpy as np
        B, L, C1, C2, K, K_IN = (4, 128, 128, 128, 32, 32)
        BN_EPS = 1e-05

        def _gated_bottleneck(x2d, conv_w, conv_b, gamma, beta, lin_w, lin_b):
            n = x2d.shape[0]
            g = conv_w.shape[0]
            xc = jnp.einsum('ngf,gf->ng', x2d.reshape(n, g, 4), conv_w) + conv_b
            mean = jnp.mean(xc, axis=0)
            var = jnp.mean((xc - mean) ** 2, axis=0)
            xn = (xc - mean) * jax.lax.rsqrt(var + BN_EPS) * gamma + beta
            xa = jax.nn.gelu(xn, approximate=False)
            return xa @ lin_w.T + lin_b
        b, l, c1 = x.shape
        c2 = weight.shape[1]
        x2d = x.reshape(b * l, c1)
        bi = jnp.arange(b)[:, None, None]
        li = jnp.arange(l)[None, :, None]
        score_out = jax.nn.softmax(_gated_bottleneck(x2d, so_conv_w, so_conv_b, so_gamma, so_beta, so_lin_w, so_lin_b).reshape(b, l, c2), axis=-1)
        s_v_out, s_i_out = jax.lax.top_k(score_out, K)
        full = jnp.einsum('blc,co->blo', x, weight)
        out_k = jnp.take_along_axis(full, s_i_out, axis=-1) * s_v_out
        out_branch = jnp.zeros((b, l, c2), x.dtype).at[bi, li, s_i_out].add(out_k)
        score_in = jax.nn.softmax(_gated_bottleneck(x2d, si_conv_w, si_conv_b, si_gamma, si_beta, si_lin_w, si_lin_b).reshape(b, l, c1), axis=-1)
        s_v_in, s_i_in = jax.lax.top_k(score_in, K_IN)
        x_gated = jnp.take_along_axis(x, s_i_in, axis=-1) * s_v_in
        x_sparse = jnp.zeros((b, l, c1), x.dtype).at[bi, li, s_i_in].add(x_gated)
        in_branch = jnp.einsum('blc,co->blo', x_sparse, weight)
        return out_branch + in_branch + bias
    x = x + _L0_xattn_ref(_layernorm(x, axis=-1), ctx_1024, ctx_1024, L0_xattn_Wq, L0_xattn_bq, L0_xattn_Wk, L0_xattn_bk, L0_xattn_Wv, L0_xattn_bv, L0_xattn_Wo, L0_xattn_bo)
    x = x + _L0_ffn_ref(_layernorm(x, axis=-1), L0_ffn_weight, L0_ffn_bias, L0_ffn_so_conv_w, L0_ffn_so_conv_b, L0_ffn_so_gamma, L0_ffn_so_beta, L0_ffn_so_lin_w, L0_ffn_so_lin_b, L0_ffn_si_conv_w, L0_ffn_si_conv_b, L0_ffn_si_gamma, L0_ffn_si_beta, L0_ffn_si_lin_w, L0_ffn_si_lin_b)
    return x

_drawn_inputs = setup_inputs


def setup_inputs(seed=0):
    import zlib

    import numpy as np

    out = dict(_drawn_inputs(seed))
    spreads = {'L0_ffn_bias': (0.0, 0.1),
     'L0_ffn_so_conv_b': (0.0, 0.8),
     'L0_ffn_so_gamma': (1.0, 0.6),
     'L0_ffn_so_beta': (0.0, 0.8),
     'L0_ffn_so_lin_b': (0.0, 0.8),
     'L0_ffn_si_conv_b': (0.0, 0.8),
     'L0_ffn_si_gamma': (1.0, 0.6),
     'L0_ffn_si_beta': (0.0, 0.8),
     'L0_ffn_si_lin_b': (0.0, 0.8)}
    factors = {'L0_xattn_bq': 8.0,
     'L0_xattn_bk': 8.0,
     'L0_xattn_bv': 5.721,
     'L0_xattn_bo': 5.754,
     'L0_ffn_weight': 3.621,
     'L0_ffn_so_conv_w': 7.024,
     'L0_ffn_so_lin_w': 6.39,
     'L0_ffn_si_conv_w': 7.011,
     'L0_ffn_si_lin_w': 6.459}
    for name, (base, spread) in spreads.items():
        noise = np.random.default_rng([zlib.crc32(name.encode()), seed]).standard_normal(out[name].shape)
        drawn = base * np.exp(spread * noise) if base else spread * noise
        out[name] = jnp.asarray(drawn.astype(out[name].dtype))
    for name, factor in factors.items():
        out[name] = (out[name] * factor).astype(out[name].dtype)
    return out
```

```python
from contextlib import ExitStack

import numpy as np

import concourse.bass as bass
from concourse import mybir

F32 = mybir.dt.float32
BF16 = mybir.dt.bfloat16
ALU = mybir.AluOpType
ACT = mybir.ActivationFunctionType
AX = mybir.AxisListType

BATCH, SEQ, DIM, HEADS = 128, 64, 128, 16
DH = DIM // HEADS
PAIRS = 4
GROUPS = BATCH // (2 * PAIRS)
TILES = GROUPS * PAIRS
GTOK = PAIRS * 2 * SEQ
HALF = PAIRS * SEQ
PARTS = 3
PRODUCTS = [(0, 0), (0, 1), (1, 0), (1, 1), (0, 2), (2, 0)]
ROWS = len(PRODUCTS) * DH
MROWS = 2 * ROWS
KROWS = MROWS + 4
VW = DH + 1
GATES = DIM // 4
TOPK = 32
LN_EPS = 1e-5
BN_EPS = 1e-5
SCALE = float(1.0 / np.sqrt(DH).astype(np.float32))
PICKED = -3.0e38
PT_RING = 4
SPLIT_DMAS = 2 * len(PRODUCTS)


class Turn:

    def __init__(self, base, reg=None):
        self.base, self.reg = base, reg

    def lin(self, off, per, extra=0):
        if self.reg is None:
            return per * (self.base + off) + extra
        return self.reg * (2 * per) + (per * (self.base + off) + extra)

    def slot(self, off):
        return (self.base + off) % 2

    def uses(self, off, per, extra=0):
        if self.reg is None:
            return per * ((self.base + off) // 2 + 1) + extra
        return self.reg * per + (per * ((self.base + off) // 2 + 1) + extra)

    def has(self, off, groups=GROUPS):
        return self.reg is not None or 0 <= self.base + off < groups


def wait(eng, sem, value):
    if isinstance(value, int) and value <= 0:
        return
    eng.wait_ge(sem, value)


def build(nc, x, ctxT, wq, wk, wv, wo, bqk, bv, bo, bf, ffn_w, conv, gate_cols, lin_w, ident, shift_rows, v_frame, out):
    with ExitStack() as ctx:
        def sb(name, shape, dt=F32):
            return ctx.enter_context(nc.sbuf_tensor(name, shape, dt))

        def ps(name, shape, dt=F32):
            return ctx.enter_context(nc.psum_tensor(name, shape, dt))

        def sem(name):
            return ctx.enter_context(nc.semaphore(name))

        xr = sb("xr", [128, TILES, DIM])
        x2all = sb("x2all", [128, TILES, DIM])
        gates = sb("gates", [2 * GATES, TILES * 128])
        qst = [sb(f"qst{s}", [128, HEADS, HALF], BF16) for s in range(2)]
        kst = [sb(f"kst{s}", [128, HEADS, 2, SEQ * PAIRS], BF16) for s in range(2)]
        cT = [sb(f"cT{s}", [128, 2 * SEQ, PAIRS]) for s in range(2)]
        xn = [sb(f"xn{s}", [128, PAIRS, DIM]) for s in range(2)]
        xnT = sb("xnT", [128, 2, PAIRS, SEQ])
        q32 = sb("q32", [128, GTOK])
        k32 = sb("k32", [128, GTOK])
        q_rest = sb("q_rest", [128, GTOK])
        k_rest = sb("k_rest", [128, GTOK])
        q_parts = sb("q_parts", [128, PARTS, GTOK], BF16)
        k_parts = sb("k_parts", [128, PARTS, GTOK], BF16)
        vx = [sb(f"vx{s}", [128, PAIRS, HEADS, 2 * VW]) for s in range(2)]
        pT = sb("pT", [128, PT_RING, HEADS // 2, SEQ])
        attn = sb("attn", [128, 2, 2, DIM])
        attnT = sb("attnT", [128, 2, 2, 2 * SEQ])
        den = sb("den", [128, 2, HEADS, 2])
        x2w = [sb(f"x2w{s}", [128, PAIRS, DIM]) for s in range(2)]
        x2T = sb("x2T", [128, GTOK])
        m32 = sb("m32", [128, 2, 2, HEADS])
        m_parts = sb("m_parts", [128, 2, 2, 2, HEADS], BF16)
        mT = sb("mT", [64, 2, 128], BF16)
        st1 = sb("st1", [128, PAIRS, 6])
        st2 = sb("st2", [128, PAIRS, 6])
        ag1 = sb("ag1", [128, PAIRS, 2])
        ag2 = sb("ag2", [128, PAIRS, 2])
        ve1 = sb("ve1", [128, PAIRS])
        ve2 = sb("ve2", [128, PAIRS])
        rs1 = sb("rs1", [128, PAIRS])
        rs2 = sb("rs2", [128, PAIRS])
        nm1 = sb("nm1", [128, PAIRS])
        nm2 = sb("nm2", [128, PAIRS])
        gate_st = sb("gate_st", [2 * GATES, GROUPS, 6])
        gate_ag = sb("gate_ag", [2 * GATES, 2])
        gate_ab = sb("gate_ab", [2 * GATES, 4])
        idf = sb("idf", [128, 128])
        idb = sb("idb", [128, 128], BF16)
        wq_sb = sb("wq_sb", [128, DIM])
        wk_sb = sb("wk_sb", [128, DIM])
        wv_sb = sb("wv_sb", [128, DIM])
        wo_sb = sb("wo_sb", [128, DIM])
        wf_sb = sb("wf_sb", [128, DIM])
        conv_sb = sb("conv_sb", [128, 2 * GATES])
        lin_sb = sb("lin_sb", [2 * GATES + 1, 2 * DIM])
        bqk_sb = sb("bqk_sb", [128, 2])
        bv_wide = sb("bv_wide", [128, 128])
        bo_row = sb("bo_row", [128, DIM])
        bf_row = sb("bf_row", [128, DIM])
        gcol = sb("gcol", [2 * GATES, 3])
        half_neg = sb("half_neg", [128, PAIRS])
        picked, expd, gated_x, full_s, y_sb, g2 = [], [], [], [], [], []
        for s in range(2):
            room = kst[s][:, :, :, :].bitcast(F32).rearrange("p h a t -> p (h a t)")
            picked.append(room[:, 0:1024].rearrange("p (t c) -> p t c", t=PAIRS))
            expd.append(room[:, 1024:2048].rearrange("p (t c) -> p t c", t=PAIRS))
            gated_x.append(room[:, 2048:2560].rearrange("p (t c) -> p t c", t=PAIRS))
            full_s.append(room[:, 2560:3072].rearrange("p (t c) -> p t c", t=PAIRS))
            y_sb.append(room[:, 3072:3584].rearrange("p (t c) -> p t c", t=PAIRS))
            g2.append(room[:, 3584:4096])
        xsT = q32
        yin = k32[:, :].rearrange("q (p c) -> q p c", p=PAIRS)
        top_first = [sb(f"top_first{s}", [128, 2 * PAIRS, 8]) for s in range(2)]
        top_next = sb("top_next", [128, 2 * PAIRS, 8])
        neg_max = [sb(f"neg_max{s}", [128, 2 * PAIRS]) for s in range(2)]
        sums = [sb(f"sums{s}", [128, 2 * PAIRS]) for s in range(2)]
        rsum = [sb(f"rsum{s}", [128, 2 * PAIRS]) for s in range(2)]

        ps_turn = ps("ps_turn", [128, GTOK])
        ps_proj = ps("ps_proj", [128, GTOK])
        ps_row = [ps(f"ps_row{i}", [128, 4, 2, SEQ]) for i in range(2)]
        ps_col = [ps(f"ps_col{i}", [128, HEADS // 2, SEQ]) for i in range(2)]
        ps_pv = ps("ps_pv", [128, 512])
        ps_mix = ps("ps_mix", [128, 512])
        ps_logits = [[b[:, :, :, :].rearrange("q h a t -> q (h a t)").rearrange("q (t c) -> q t c", t=2) for b in ps_row],
                     [b[:, :, :].rearrange("q h t -> q (h t)").rearrange("q (t c) -> q t c", t=2) for b in ps_col]]
        pv_view = ps_pv[:, 0:HEADS * 2 * VW].rearrange("q (h a v) -> q h a v", a=2, v=VW)

        consts_in = sem("consts_in")
        x_in = [sem(f"x_in{s}") for s in range(2)]
        ctx_in = [sem(f"ctx_in{s}") for s in range(2)]
        q_moved = [sem(f"q_moved{s}") for s in range(2)]
        k_moved = [sem(f"k_moved{s}") for s in range(2)]
        m_moved = [[sem(f"m_moved{h}{s}") for s in range(2)] for h in range(2)]
        x2_kept = [sem(f"x2_kept{s}") for s in range(2)]
        pe_xT, pe_q, pe_k, pe_v = sem("pe_xT"), sem("pe_q"), sem("pe_k"), sem("pe_v")
        pe_row, pe_col, pe_pv = sem("pe_row"), sem("pe_col"), sem("pe_pv")
        pe_mT, pe_attnT, pe_out = sem("pe_mT"), sem("pe_attnT"), sem("pe_out")
        pe_x2T, pe_conv, pe_bias = sem("pe_x2T"), sem("pe_conv"), sem("pe_bias")
        act_ln1, act_xT, act_q, act_k, act_v = (sem(f"act_{n}") for n in ("ln1", "xT", "q", "k", "v"))
        act_mT, act_exp, act_attnT = sem("act_mT"), sem("act_exp"), sem("act_attnT")
        act_ln2, act_x2T, act_conv, act_gelu = (sem(f"act_{n}") for n in ("ln2", "x2T", "conv", "gelu"))
        dve_st1, dve_ag1, dve_st2, dve_ag2 = (sem(f"dve_{n}") for n in ("st1", "ag1", "st2", "ag2"))
        dve_max, dve_mhi, dve_m = sem("dve_max"), sem("dve_mhi"), sem("dve_m")
        dve_den, dve_attn, dve_x1, dve_gate = (sem(f"dve_{n}") for n in ("den", "attn", "x1", "gate"))
        dve_split = sem("dve_split")
        dve_bias, dve_setup = sem("dve_bias"), sem("dve_setup")
        gp_rs1, gp_rs2, gp_split, gp_xb, gp_bn = (sem(f"gp_{n}") for n in ("rs1", "rs2", "split", "xb", "bn"))
        g_in = [sem(f"g_in{s}") for s in range(2)]
        x2_in = [sem(f"x2_in{s}") for s in range(2)]
        p2_x2T, p2_lin, p2_full, p2_xsT, p2_yin = (sem(f"p2_{n}") for n in ("x2T", "lin", "full", "xsT", "yin"))
        a2_x2T, a2_exp, a2_left, a2_full, a2_xsT, a2_yin = (sem(f"a2_{n}") for n in ("x2T", "exp", "left", "full", "xsT", "yin"))
        d2_max, d2_rep, d2_rsum = sem("d2_max"), sem("d2_rep"), sem("d2_rsum")
        g2_neg, g2_gate, g2_xs, g2_sum = (sem(f"g2_{n}") for n in ("neg", "gate", "xs", "sum"))
        out_done = [sem(f"out_done{s}") for s in range(2)]
        passed = sem("passed")

        def hold(eng, semaphore, value):
            if isinstance(value, int):
                wait(eng, semaphore, value)
            else:
                eng.wait_ge(semaphore, value)
                eng.sem_inc(passed, 1)

        CONSTS = 13 + 2 * 2
        FIRST, LAST = -2, GROUPS + 1

        def run(eng, turn):
            for i in range(FIRST, 4):
                turn(Turn(i))
            with eng.Fori(0, (GROUPS - 8) // 2) as j:
                turn(Turn(4, j))
                turn(Turn(5, j))
            for i in range(GROUPS - 4, LAST + 1):
                turn(Turn(i))

        def run2(eng, turn):
            for i in range(3):
                turn(Turn(i))
            with eng.Fori(0, (GROUPS - 4) // 2) as j:
                turn(Turn(3, j))
                turn(Turn(4, j))
            turn(Turn(GROUPS - 1))
            turn(Turn(GROUPS))

        def tiles_of(tensor, t, off):
            if t.reg is not None:
                return tensor[:, bass.ds(t.lin(off, PAIRS), PAIRS), :]
            g = t.base + off
            return tensor[:, PAIRS * g:PAIRS * (g + 1), :]

        def split(eng, whole, rest, parts, done, t):
            hold(eng, done, t.lin(1, 4))
            eng.tensor_copy(parts[:, 0, :], whole[:, :]).then_inc(done, 1)
            hold(eng, done, t.lin(1, 4, 1))
            eng.tensor_tensor(rest[:, :], whole[:, :], parts[:, 0, :], ALU.subtract).then_inc(done, 1)
            hold(eng, done, t.lin(1, 4, 2))
            eng.tensor_copy(parts[:, 1, :], rest[:, :]).then_inc(done, 1)
            hold(eng, done, t.lin(1, 4, 3))
            eng.tensor_tensor(parts[:, 2, :], rest[:, :], parts[:, 1, :], ALU.subtract).then_inc(done, 1)

        block = ctx.enter_context(nc.Block())

        @block.sync
        def _(sp):
            for dst, src in ((idf, ident), (wq_sb, wq), (wk_sb, wk), (wv_sb, wv), (wo_sb, wo), (wf_sb, ffn_w),
                             (conv_sb, conv), (lin_sb, lin_w), (bqk_sb, bqk), (gcol, gate_cols),
                             (bv_wide, bv), (bo_row, bo), (bf_row, bf)):
                sp.dma_start(dst[:, :], src).then_inc(consts_in, 16)
            for s in range(2):
                sp.dma_start(xr[:, PAIRS * s:PAIRS * (s + 1), :], x[:, PAIRS * s:PAIRS * (s + 1), :]).then_inc(x_in[s], 16)
                sp.dma_start(cT[s][:, :, :], ctxT[:, s]).then_inc(ctx_in[s], 16)
            for s in range(2):
                sp.dma_start(vx[s][:, :, :, :].rearrange("k p h v -> k (p h v)"), v_frame).then_inc(consts_in, 16)
                sp.dma_start(kst[s][0:KROWS, :, :, :].rearrange("r h a t -> r (h a t)"), shift_rows).then_inc(consts_in, 16)

            def turn(t):
                if t.has(4):
                    hold(sp, dve_ag1, t.lin(3, 1))
                    sp.dma_start(tiles_of(xr, t, 4), tiles_of(x, t, 4)).then_inc(x_in[t.slot(4)], 16)
                if t.has(-2):
                    hold(sp, act_ln2, t.lin(-1, 1))
                    sp.dma_start(tiles_of(x2all, t, -2), x2w[t.slot(-2)][:, :, :]).then_inc(x2_kept[t.slot(-2)], 16)
                if t.has(0):
                    for h in range(2):
                        hold(sp, act_mT, t.lin(0, 2, h + 1))
                        hold(sp, pe_col, t.lin(-1, 8))
                        sp.dma_start(qst[t.slot(0)][MROWS:KROWS, :, h * 128:(h + 1) * 128],
                                     mT[:, h, :]).then_inc(m_moved[h][t.slot(0)], 16)
                if t.has(3) and t.base + 3 >= 2:
                    hold(sp, pe_v, t.lin(2, 1))
                    sp.dma_start(cT[t.slot(3)][:, :, :], ctxT[:, bass.ds(t.lin(3, 1), 1)].rearrange("c g m p -> c (g m) p")
                                 if t.reg is not None else ctxT[:, t.base + 3]).then_inc(ctx_in[t.slot(3)], 16)
                if t.has(1):
                    s = t.slot(1)
                    for parts, stacked, sems, ready, side in ((q_parts, qst, q_moved, dve_split, 0),
                                                              (k_parts, kst, k_moved, gp_split, 1)):
                        hold(sp, ready, t.lin(2, 4))
                        hold(sp, pe_col, t.lin(0, 8))
                        for n, pair in enumerate(PRODUCTS):
                            for a in range(2):
                                r = a * ROWS + n * DH
                                dst = stacked[s][r:r + DH, :, :] if side == 0 else stacked[s][r:r + DH, :, a, :]
                                sp.dma_start(dst, parts[:, pair[side], a * HALF:(a + 1) * HALF]).then_inc(sems[s], 16)

            run(sp, turn)

            def turn2(t):
                if t.has(0):
                    s = t.slot(0)
                    hold(sp, p2_lin, t.lin(-1, 1))
                    g0 = t.lin(0, GTOK)
                    hold(sp, act_gelu, 4)
                    sp.dma_start(g2[s][0:2 * GATES, :], gates[:, bass.ds(g0, GTOK)] if t.reg is not None
                                 else gates[:, g0:g0 + GTOK]).then_inc(g_in[s], 16)
                    hold(sp, g2_xs, t.lin(-1, 1))
                    hold(sp, p2_x2T, t.lin(-1, 1))
                    sp.dma_start(x2w[s][:, :, :], tiles_of(x2all, t, 0)).then_inc(x2_in[s], 16)
                if t.has(-1):
                    s = t.slot(-1)
                    hold(sp, g2_sum, t.lin(-1, 4, 4))
                    sp.dma_start(tiles_of(out, t, -1), y_sb[s][:, :, :]).then_inc(out_done[s], 16)

            for s in range(2):
                sp.wait_ge(x2_kept[s], 16 * GROUPS // 2)
            run2(sp, turn2)
            for s in range(2):
                sp.wait_ge(out_done[s], 16 * GROUPS // 2)

        @block.tensor
        def _(pe):
            pe.wait_ge(consts_in, 16 * CONSTS)
            pe.wait_ge(dve_setup, 3)
            pe.matmul(ps_mix[:, 0:DIM], bv_wide[:, :], wo_sb[:, :], start=True, stop=True).then_inc(pe_bias, 1)

            def k_cols(s, rows, h, p):
                return kst[s][0:rows, h, :, :].rearrange("r a (m p) -> r (a m) p", p=PAIRS)[:, :, p]

            def key_side(t, p):
                s = t.slot(-1)
                if p % 2 == 0:
                    wait(pe, m_moved[p // 2][s], t.uses(-1, 16))
                for b in range(2):
                    wait(pe, act_exp, t.lin(-1, 8, 2 * p + b - 1))
                    for hh in range(HEADS // 2):
                        h = b * (HEADS // 2) + hh
                        mm = pe.matmul(ps_col[b][:, hh, :], k_cols(s, KROWS, h, p),
                                       qst[s][0:KROWS, h, p * SEQ:(p + 1) * SEQ], start=True, stop=True)
                    mm.then_inc(pe_col, 1)

            def values(t, p):
                s, pp = t.slot(-1), p % 2
                wait(pe, act_exp, t.lin(-1, 8, 2 * p + 2))
                if p == 0:
                    wait(pe, act_v, t.lin(0, 1))
                if pp == 0:
                    wait(pe, dve_attn, t.lin(-1, 2, p // 2))
                for h in range(HEADS):
                    half = 2 * p + h // (HEADS // 2)
                    mm = pe.matmul(ps_pv[pp * SEQ:(pp + 1) * SEQ, h * 2 * VW:(h + 1) * 2 * VW],
                                   pT[:, half % PT_RING, h % (HEADS // 2), :], vx[s][:, p, h, :], start=True, stop=True)
                mm.then_inc(pe_pv, 1)

            def turn_attn(t, hp):
                wait(pe, dve_attn, t.lin(-1, 2, hp + 1))
                wait(pe, dve_x1, t.lin(-1, 2, hp))
                if t.has(0) and hp == 1:
                    wait(pe, act_mT, t.lin(0, 2, 1))
                for a in range(2):
                    mm = pe.transpose(ps_mix[:, a * 128:(a + 1) * 128], attn[:, hp, a, :], idf[:, :])
                mm.then_inc(pe_attnT, 1)

            def out_proj(t, hp):
                wait(pe, act_attnT, t.lin(-1, 2, hp + 1))
                if t.has(0) and hp == 1:
                    wait(pe, act_mT, t.lin(0, 2, 2))
                for pp in range(2):
                    mm = pe.matmul(ps_mix[:, pp * DIM:(pp + 1) * DIM], attnT[:, hp, pp, :], wo_sb[:, :],
                                   start=True, stop=True)
                mm.then_inc(pe_out, 1)

            def query_side(t, b):
                s, hp, j = t.slot(0), b // 4, b % 4
                if b == 0:
                    wait(pe, q_moved[s], t.uses(0, 16 * SPLIT_DMAS))
                    wait(pe, k_moved[s], t.uses(0, 16 * SPLIT_DMAS))
                wait(pe, dve_max, t.lin(0, 8, b - 1))
                for hh in range(4):
                    h = 4 * j + hh
                    for pp in range(2):
                        p = 2 * hp + pp
                        mm = pe.matmul(ps_row[b % 2][pp * SEQ:(pp + 1) * SEQ, hh, :, :],
                                       qst[s][0:MROWS, h, p * SEQ:(p + 1) * SEQ],
                                       k_cols(s, MROWS, h, p), start=True, stop=True)
                mm.then_inc(pe_row, 1)

            def turn_max(t, hp):
                hold(pe, dve_m, t.lin(0, 2, hp + 1))
                if t.has(-1):
                    if hp == 0:
                        hold(pe, dve_x1, t.lin(-1, 2, 1))
                    else:
                        hold(pe, act_attnT, t.lin(-1, 2, 2))
                else:
                    hold(pe, act_mT, t.lin(0, 2, hp))
                pe.transpose(ps_mix[0:64, 0:64].bitcast(BF16), m_parts[:, hp, :, :, :].rearrange("q a x h -> q (a x h)"),
                             idb[:, :]).then_inc(pe_mT, 1)

            def turn(t):
                c, d, a, r = t.has(-1), t.has(-2), t.has(1), t.has(0)
                if c:
                    key_side(t, 0)
                    key_side(t, 1)
                    values(t, 0)
                    key_side(t, 2)
                    values(t, 1)
                if d:
                    wait(pe, act_ln2, t.lin(-1, 1))
                    wait(pe, act_xT, t.lin(1, 1) if a or r or t.reg is not None else GROUPS)
                    for p in range(PAIRS):
                        mm = pe.transpose(ps_turn[:, p * 128:(p + 1) * 128], x2w[t.slot(-2)][:, p, :], idf[:, :])
                    mm.then_inc(pe_x2T, 1)
                if c:
                    key_side(t, 3)
                    turn_attn(t, 0)
                    values(t, 2)
                    out_proj(t, 0)
                    values(t, 3)
                if d:
                    wait(pe, act_x2T, t.lin(-1, 1))
                    wait(pe, act_v, t.lin(1, 1) if r or t.reg is not None else GROUPS)
                    wait(pe, act_conv, t.lin(-2, 1))
                    pe.matmul(ps_proj[0:2 * GATES, :], conv_sb[:, :], x2T[:, :], start=True, stop=True).then_inc(pe_conv, 1)
                if a:
                    wait(pe, act_ln1, t.lin(2, 1))
                    wait(pe, act_x2T, t.lin(-1, 1))
                    wait(pe, act_xT, t.lin(1, 1))
                    for p in range(PAIRS):
                        mm = pe.transpose(ps_turn[:, p * 128:(p + 1) * 128], xn[t.slot(1)][:, p, :], idf[:, :])
                    mm.then_inc(pe_xT, 1)
                if r:
                    for b in range(6):
                        query_side(t, b)
                    turn_max(t, 0)
                    query_side(t, 6)
                    query_side(t, 7)
                if a:
                    wait(pe, act_xT, t.lin(2, 1))
                    wait(pe, act_conv, t.lin(-1, 1))
                    wait(pe, act_v, t.lin(1, 1))
                    pe.matmul(ps_proj[:, :], wq_sb[:, :], xnT[:, :, :, :].rearrange("c a p s -> c (a p s)"),
                              start=True, stop=True).then_inc(pe_q, 1)
                if c:
                    turn_attn(t, 1)
                if a:
                    wait(pe, ctx_in[t.slot(1)], t.uses(1, 16))
                    wait(pe, act_q, t.lin(2, 1))
                    pe.matmul(ps_proj[:, :], wk_sb[:, :], cT[t.slot(1)][:, :, :].rearrange("c m p -> c (m p)"),
                              start=True, stop=True).then_inc(pe_k, 1)
                if r:
                    turn_max(t, 1)
                if c:
                    out_proj(t, 1)
                if a:
                    wait(pe, act_k, t.lin(2, 1))
                    for p in range(PAIRS):
                        mm = pe.matmul(ps_proj[:, p * DIM:(p + 1) * DIM], cT[t.slot(1)][:, :, p], wv_sb[:, :],
                                       start=True, stop=True)
                    mm.then_inc(pe_v, 1)

            run(pe, turn)

            def turn2(t):
                if t.has(0):
                    s = t.slot(0)
                    logits = ps_logits[s]
                    wait(pe, x2_in[s], t.uses(0, 16))
                    wait(pe, a2_x2T, t.lin(0, 1))
                    for p in range(PAIRS):
                        mm = pe.transpose(ps_turn[:, p * 128:(p + 1) * 128], x2w[s][:, p, :], idf[:, :])
                    mm.then_inc(p2_x2T, 1)
                    wait(pe, g_in[s], t.uses(0, 16))
                    if t.base == 0 and t.reg is None:
                        wait(pe, gp_bn, 8)
                    wait(pe, a2_exp, t.lin(-1, 1))
                    wait(pe, d2_rep, t.lin(-1, 4))
                    for p in range(PAIRS):
                        mm = pe.matmul(logits[p // 2][:, p % 2, :], g2[s][0:2 * GATES + 1, p * 128:(p + 1) * 128], lin_sb[:, :],
                                       start=True, stop=True)
                    mm.then_inc(p2_lin, 1)
                    wait(pe, a2_x2T, t.lin(1, 1))
                    wait(pe, a2_full, t.lin(0, 1))
                    for p in range(PAIRS):
                        mm = pe.matmul(ps_proj[:, p * DIM:(p + 1) * DIM], x2T[:, p * 128:(p + 1) * 128], wf_sb[:, :],
                                       start=True, stop=True)
                    mm.then_inc(p2_full, 1)
                if t.has(-1):
                    s = t.slot(-1)
                    wait(pe, g2_xs, t.lin(0, 1))
                    wait(pe, a2_xsT, t.lin(-1, 1))
                    for p in range(PAIRS):
                        mm = pe.transpose(ps_pv[:, p * 128:(p + 1) * 128], gated_x[s][:, p, :], idf[:, :])
                    mm.then_inc(p2_xsT, 1)
                    wait(pe, a2_xsT, t.lin(0, 1))
                    wait(pe, a2_yin, t.lin(-1, 1))
                    for p in range(PAIRS):
                        mm = pe.matmul(ps_mix[:, p * DIM:(p + 1) * DIM], xsT[:, p * 128:(p + 1) * 128], wf_sb[:, :],
                                       start=True, stop=True)
                    mm.then_inc(p2_yin, 1)

            run2(pe, turn2)

        @block.scalar
        def _(act):
            act.wait_ge(consts_in, 16 * CONSTS)

            def exp_half(t, b):
                wait(act, pe_col, t.lin(-1, 8, b + 1))
                wait(act, pe_pv, t.lin(-1, 4, (b - PT_RING) // 2 + 1))
                act.activation(pT[:, b % PT_RING, :, :], ps_col[b % 2][:, :, :], ACT.Exp, scale=SCALE).then_inc(act_exp, 1)

            def norm(t, off, src, dst, rs, nm):
                for p in range(PAIRS):
                    tile = src[:, bass.ds(t.lin(off, PAIRS, p), 1), :].rearrange("q o c -> q (o c)") if t.reg is not None \
                        else src[:, PAIRS * (t.base + off) + p, :]
                    ins = act.activation(dst[:, p, :], tile, ACT.Identity, bias=nm[:, p:p + 1], scale=rs[:, p:p + 1])
                return ins

            def attn_out(t, hp):
                wait(act, pe_attnT, t.lin(-1, 2, hp + 1))
                act.activation(attnT[:, hp, :, :].rearrange("d p (a s) -> d a p s", a=2),
                               ps_mix[:, 0:256].rearrange("d (a p s) -> d a p s", a=2, p=2), ACT.Copy).then_inc(act_attnT, 1)

            def max_out(t, hp):
                wait(act, pe_mT, t.lin(0, 2, hp + 1))
                wait(act, m_moved[hp][t.slot(-1)], t.uses(-1, 16))
                act.activation(mT[:, hp, :], ps_mix[0:64, 0:64].bitcast(BF16), ACT.Copy).then_inc(act_mT, 1)

            def turn(t):
                c, d, a, r = t.has(-1), t.has(-2), t.has(1), t.has(0)
                for b in range(8):
                    if c:
                        exp_half(t, b)
                    if b == 3 and d:
                        wait(act, gp_rs2, t.lin(-1, 4))
                        wait(act, x2_kept[t.slot(-4)], t.uses(-4, 16))
                        norm(t, -2, xr, x2w[t.slot(-2)], rs2, nm2).then_inc(act_ln2, 1)
                    if b == 6:
                        if d:
                            wait(act, pe_x2T, t.lin(-1, 1))
                            wait(act, pe_conv, t.lin(-2, 1))
                            act.activation(x2T[:, :], ps_turn[:, :], ACT.Copy).then_inc(act_x2T, 1)
                        if c:
                            attn_out(t, 0)
                if d:
                    wait(act, pe_conv, t.lin(-1, 1))
                    g0 = t.lin(-2, GTOK)
                    act.activation(gates[:, bass.ds(g0, GTOK)] if t.reg is not None else gates[:, g0:g0 + GTOK],
                                   ps_proj[0:2 * GATES, :], ACT.Identity, bias=gcol[:, 0:1]).then_inc(act_conv, 1)
                if a:
                    wait(act, pe_xT, t.lin(2, 1))
                    wait(act, pe_q, t.lin(1, 1))
                    act.activation(xnT[:, :, :, :], ps_turn[:, :].rearrange("c (p a s) -> c a p s", a=2, s=SEQ),
                                   ACT.Copy).then_inc(act_xT, 1)
                if r:
                    max_out(t, 0)
                if a:
                    wait(act, pe_q, t.lin(2, 1))
                    wait(act, dve_split, t.lin(1, 4))
                    act.activation(q32[:, :], ps_proj[:, :], ACT.Identity, bias=bqk_sb[:, 0:1]).then_inc(act_q, 1)
                if c:
                    attn_out(t, 1)
                if a:
                    wait(act, pe_k, t.lin(2, 1))
                    wait(act, gp_split, t.lin(1, 4))
                    act.activation(k32[:, :], ps_proj[:, :], ACT.Identity, bias=bqk_sb[:, 1:2]).then_inc(act_k, 1)
                if r:
                    max_out(t, 1)
                if a:
                    s = t.slot(1)
                    wait(act, pe_v, t.lin(2, 1))
                    wait(act, pe_pv, t.lin(0, 4))
                    for half in range(2):
                        rows = slice(half * SEQ, (half + 1) * SEQ)
                        ins = act.activation(vx[s][rows, :, :, half * VW:half * VW + DH],
                                             ps_proj[rows, :].rearrange("k (p h i) -> k p h i", p=PAIRS, i=DH), ACT.Copy)
                    ins.then_inc(act_v, 1)
                if t.has(2):
                    wait(act, gp_rs1, t.lin(3, 4))
                    wait(act, pe_xT, t.lin(1, 1))
                    norm(t, 2, xr, xn[t.slot(2)], rs1, nm1).then_inc(act_ln1, 1)

            run(act, turn)

            act.wait_ge(act_conv, GROUPS)
            act.wait_ge(gp_bn, 5)
            for n in range(4):
                part = gates[:, n * TILES * 32:(n + 1) * TILES * 32]
                act.activation(part, part, ACT.Gelu, bias=gate_ab[:, 3:4], scale=gate_ab[:, 2:3]).then_inc(act_gelu, 1)

            def turn2(t):
                if t.has(0):
                    s = t.slot(0)
                    wait(act, p2_x2T, t.lin(1, 1))
                    wait(act, p2_full, t.lin(0, 1))
                    act.activation(x2T[:, :], ps_turn[:, :], ACT.Copy).then_inc(a2_x2T, 1)
                    wait(act, g2_neg, t.lin(1, 1))
                    wait(act, d2_rep, t.lin(0, 4, 1))
                    wait(act, g2_sum, t.lin(-1, 4))
                    wait(act, d2_rsum, t.lin(-1, 1))
                    for p in range(PAIRS):
                        for gate in range(2):
                            n = 2 * p + gate
                            ins = act.activation(expd[s][:, p, gate * DIM:(gate + 1) * DIM],
                                                 ps_logits[s][p // 2][:, p % 2, gate * DIM:(gate + 1) * DIM], ACT.Exp,
                                                 bias=neg_max[s][:, n:n + 1], accum_out=sums[s][:, n:n + 1])
                    ins.then_inc(a2_exp, 1)
                if t.has(-1):
                    s = t.slot(-1)
                    wait(act, d2_rep, t.lin(0, 4))
                    for p in range(PAIRS):
                        for gate in range(2):
                            tile = picked[s][:, p, gate * DIM:(gate + 1) * DIM]
                            n = 2 * p + gate
                            ins = act.activation(tile, tile, ACT.Exp, bias=neg_max[s][:, n:n + 1])
                    ins.then_inc(a2_left, 1)
                    wait(act, p2_xsT, t.lin(0, 1))
                    wait(act, p2_yin, t.lin(-1, 1))
                    act.activation(xsT[:, :], ps_pv[:, :], ACT.Copy).then_inc(a2_xsT, 1)
                    wait(act, p2_yin, t.lin(0, 1))
                    wait(act, g2_sum, t.lin(-1, 4))
                    for p in range(PAIRS):
                        ins = act.activation(yin[:, p, :], ps_mix[:, p * DIM:(p + 1) * DIM], ACT.Copy,
                                             scale=rsum[s][:, 2 * p + 1:2 * p + 2])
                    ins.then_inc(a2_yin, 1)
                if t.has(0):
                    s = t.slot(0)
                    wait(act, p2_full, t.lin(1, 1))
                    wait(act, d2_rsum, t.lin(1, 1))
                    for p in range(PAIRS):
                        ins = act.activation(full_s[s][:, p, :], ps_proj[:, p * DIM:(p + 1) * DIM], ACT.Copy,
                                             scale=rsum[s][:, 2 * p:2 * p + 1])
                    ins.then_inc(a2_full, 1)

            run2(act, turn2)

        @block.vector
        def _(dve):
            dve.memset(half_neg[:, :], -0.5).then_inc(dve_setup, 1)
            dve.wait_ge(consts_in, 16 * CONSTS)
            dve.tensor_copy(idb[:, :], idf[:, :]).then_inc(dve_setup, 1)
            dve.memset(top_next[:, :, :], 0.0).then_inc(dve_setup, 1)
            dve.wait_ge(pe_bias, 1)
            dve.tensor_tensor(bo_row[:, :], bo_row[:, :], ps_mix[:, 0:DIM], ALU.add).then_inc(dve_bias, 1)

            def stats(t, off, st, ag, st_sem, ag_sem, used, used_count):
                hold(dve, ag_sem, t.lin(off, 1))
                for p in range(PAIRS):
                    tile = xr[:, bass.ds(t.lin(off, PAIRS, p), 1), :].rearrange("q o c -> q (o c)") if t.reg is not None \
                        else xr[:, PAIRS * (t.base + off) + p, :]
                    ins = dve.bn_stats(st[:, p, :], tile)
                ins.then_inc(st_sem, 1)
                hold(dve, used, used_count)
                hold(dve, st_sem, t.lin(off + 1, 1))
                for p in range(PAIRS):
                    ins = dve.bn_aggr(ag[:, p, :], st[:, p, :])
                ins.then_inc(ag_sem, 1)

            def normalise(t, hp):
                hold(dve, pe_pv, t.lin(-1, 4, 2 * hp + 2))
                hold(dve, dve_attn, t.lin(-2, 2, hp + 1))
                dve.reciprocal(den[:, hp, :, :], pv_view[:, :, :, DH]).then_inc(dve_den, 1)
                hold(dve, pe_attnT, t.lin(-2, 2, hp + 1))
                hold(dve, dve_den, t.lin(-1, 2, hp + 1))
                for a in range(2):
                    ins = dve.tensor_tensor(attn[:, hp, a, :].rearrange("q (h i) -> q h i", i=DH), pv_view[:, :, a, 0:DH],
                                            den[:, hp, :, a].unsqueeze(2).broadcast_to([128, HEADS, DH]), ALU.mult)
                ins.then_inc(dve_attn, 1)

            def residual(t, hp):
                hold(dve, pe_out, t.lin(-1, 2, hp + 1))
                hold(dve, gp_xb, t.lin(0, 1))
                tiles = xr[:, bass.ds(t.lin(-1, PAIRS, 2 * hp), 2), :] if t.reg is not None \
                    else xr[:, PAIRS * (t.base - 1) + 2 * hp:PAIRS * (t.base - 1) + 2 * hp + 2, :]
                dve.tensor_tensor(tiles, tiles, ps_mix[:, 0:2 * DIM].rearrange("q (p c) -> q p c", p=2),
                                  ALU.add).then_inc(dve_x1, 1)

            def row_max(t, b):
                hold(dve, pe_row, t.lin(0, 8, b + 1))
                j = b % 4
                if j == 0:
                    hold(dve, dve_m, t.lin(-1, 2, b // 4 + 1))
                dve.tensor_reduce(m32[:, b // 4, :, 4 * j:4 * j + 4].rearrange("q a h -> q h a"), ps_row[b % 2][:, :, :, :],
                                  AX.X, ALU.max).then_inc(dve_max, 1)

            def max_parts(t, hp):
                hold(dve, dve_max, t.lin(0, 8, 4 * hp + 4))
                hold(dve, pe_mT, t.lin(-1, 2, hp + 1))
                dve.tensor_copy(m_parts[:, hp, :, 0, :], m32[:, hp, :, :]).then_inc(dve_mhi, 1)
                hold(dve, dve_mhi, t.lin(0, 2, hp + 1))
                dve.tensor_tensor(m_parts[:, hp, :, 1, :], m32[:, hp, :, :], m_parts[:, hp, :, 0, :],
                                  ALU.subtract).then_inc(dve_m, 1)

            def turn(t):
                c, d, a, r = t.has(-1), t.has(-2), t.has(1), t.has(0)
                if d:
                    hold(dve, dve_x1, t.lin(-1, 2))
                    stats(t, -2, st2, ag2, dve_st2, dve_ag2, gp_rs2, t.lin(-2, 4))
                if t.has(2):
                    hold(dve, x_in[t.slot(2)], t.uses(2, 16))
                    stats(t, 2, st1, ag1, dve_st1, dve_ag1, gp_rs1, t.lin(2, 4))
                if c:
                    normalise(t, 0)
                    residual(t, 0)
                    normalise(t, 1)
                if d:
                    hold(dve, act_conv, t.lin(-1, 1))
                    if t.reg is not None:
                        dve.bn_stats(gate_st[:, bass.ds(t.lin(-2, 1), 1), :].rearrange("c o n -> c (o n)"),
                                     gates[:, bass.ds(t.lin(-2, GTOK), GTOK)]).then_inc(dve_gate, 1)
                    else:
                        g = t.base - 2
                        dve.bn_stats(gate_st[:, g, :], gates[:, g * GTOK:(g + 1) * GTOK]).then_inc(dve_gate, 1)
                if r:
                    for b in range(4):
                        row_max(t, b)
                    max_parts(t, 0)
                    for b in range(4, 8):
                        row_max(t, b)
                    max_parts(t, 1)
                if c:
                    residual(t, 1)
                if a:
                    hold(dve, act_q, t.lin(2, 1))
                    hold(dve, q_moved[t.slot(0)], t.uses(0, 16 * SPLIT_DMAS))
                    split(dve, q32, q_rest, q_parts, dve_split, t)

            run(dve, turn)

            dve.wait_ge(dve_gate, GROUPS)
            dve.bn_aggr(gate_ag[:, :], gate_st[:, :, :].rearrange("c g n -> c (g n)")).then_inc(dve_gate, 1)

            def turn2(t):
                if t.has(0):
                    s = t.slot(0)
                    chains = [(2 * p + gate, p, gate) for p in range(PAIRS) for gate in range(2)]
                    hold(dve, p2_lin, t.lin(1, 1))
                    hold(dve, g2_gate, t.lin(-1, 1))
                    hold(dve, g2_neg, t.lin(-1, 1))
                    for rnd in range(TOPK // 8):
                        top = top_first[s] if rnd == 0 else top_next
                        if rnd:
                            hold(dve, d2_rep, t.lin(0, 4, rnd))
                        for n, p, gate in chains:
                            cols = slice(gate * DIM, (gate + 1) * DIM)
                            src = ps_logits[s][p // 2][:, p % 2, cols] if rnd == 0 else picked[s][:, p, cols]
                            ins = dve.max(top[:, n, :], src)
                        ins.then_inc(d2_max, 1)
                        hold(dve, d2_max, t.lin(0, 4, rnd + 1))
                        for n, p, gate in chains:
                            cols = slice(gate * DIM, (gate + 1) * DIM)
                            src = ps_logits[s][p // 2][:, p % 2, cols] if rnd == 0 else picked[s][:, p, cols]
                            ins = dve.match_replace(picked[s][:, p, cols], top[:, n, :], src, PICKED)
                        ins.then_inc(d2_rep, 1)
                        if rnd == 1:
                            hold(dve, a2_exp, t.lin(1, 1))
                            hold(dve, a2_yin, t.lin(-1, 1))
                            dve.reciprocal(rsum[s][:, :], sums[s][:, :]).then_inc(d2_rsum, 1)

            run2(dve, turn2)

        @block.gpsimd
        def _(pool):
            pool.wait_ge(dve_setup, 1)

            def rstd(t, off, ag, ve, rs, nm, ready, out_sem, used):
                hold(pool, out_sem, t.lin(off, 4))
                hold(pool, ready, t.lin(off + 1, 1))
                pool.tensor_scalar(ve[:, :], ag[:, :, 1], LN_EPS, None, ALU.add).then_inc(out_sem, 1)
                hold(pool, used, t.lin(off, 1))
                hold(pool, out_sem, t.lin(off, 4, 1))
                pool.tensor_tensor(rs[:, :], ve[:, :], half_neg[:, :], ALU.pow).then_inc(out_sem, 1)
                hold(pool, out_sem, t.lin(off, 4, 2))
                pool.tensor_tensor(nm[:, :], ag[:, :, 0], rs[:, :], ALU.mult).then_inc(out_sem, 1)
                hold(pool, out_sem, t.lin(off, 4, 3))
                pool.tensor_scalar(nm[:, :], nm[:, :], -1.0, None, ALU.mult).then_inc(out_sem, 1)

            def turn(t):
                if t.has(-2):
                    rstd(t, -2, ag2, ve2, rs2, nm2, dve_ag2, gp_rs2, act_ln2)
                if t.has(2):
                    rstd(t, 2, ag1, ve1, rs1, nm1, dve_ag1, gp_rs1, act_ln1)
                if t.has(1):
                    if t.base == -1 and t.reg is None:
                        pool.wait_ge(dve_bias, 1)
                    hold(pool, act_ln1, t.lin(2, 1))
                    tiles = tiles_of(xr, t, 1)
                    pool.tensor_tensor(tiles, tiles, bo_row[:, :].unsqueeze(1).broadcast_to([128, PAIRS, DIM]),
                                       ALU.add).then_inc(gp_xb, 1)
                    hold(pool, act_k, t.lin(2, 1))
                    hold(pool, k_moved[t.slot(0)], t.uses(0, 16 * SPLIT_DMAS))
                    split(pool, k32, k_rest, k_parts, gp_split, t)

            run(pool, turn)

            pool.wait_ge(dve_gate, GROUPS + 1)
            pool.tensor_scalar(gate_ab[:, 0:1], gate_ag[:, 1:2], BN_EPS, None, ALU.add).then_inc(gp_bn, 1)
            pool.wait_ge(gp_bn, 1)
            pool.tensor_tensor(gate_ab[:, 1:2], gate_ab[:, 0:1], half_neg[0:2 * GATES, 0:1], ALU.pow).then_inc(gp_bn, 1)
            pool.wait_ge(gp_bn, 2)
            pool.tensor_tensor(gate_ab[:, 2:3], gate_ab[:, 1:2], gcol[:, 1:2], ALU.mult).then_inc(gp_bn, 1)
            pool.wait_ge(gp_bn, 3)
            pool.tensor_tensor(gate_ab[:, 0:1], gate_ab[:, 2:3], gate_ag[:, 0:1], ALU.mult).then_inc(gp_bn, 1)
            pool.wait_ge(gp_bn, 4)
            pool.tensor_tensor(gate_ab[:, 3:4], gcol[:, 2:3], gate_ab[:, 0:1], ALU.subtract).then_inc(gp_bn, 1)
            pool.wait_ge(pe_col, 8 * GROUPS)
            for s in range(2):
                pool.memset(g2[s][2 * GATES:2 * GATES + 1, :], 1.0).then_inc(gp_bn, 1)
            pool.wait_ge(gp_bn, 7)
            pool.tensor_copy(half_neg[:, 0:1], half_neg[:, 1:2]).then_inc(gp_bn, 1)

            def turn2(t):
                if t.has(0):
                    s = t.slot(0)
                    hold(pool, d2_max, t.lin(0, 4, 1))
                    hold(pool, a2_left, t.lin(-1, 1))
                    pool.tensor_scalar(neg_max[s][:, :], top_first[s][:, :, 0], -1.0, None, ALU.mult).then_inc(g2_neg, 1)
                if t.has(-1):
                    s = t.slot(-1)
                    hold(pool, a2_left, t.lin(0, 1))
                    pool.tensor_tensor(expd[s][:, :, :], expd[s][:, :, :], picked[s][:, :, :],
                                       ALU.subtract).then_inc(g2_gate, 1)
                    hold(pool, g2_gate, t.lin(0, 1))
                    pool.tensor_tensor(gated_x[s][:, :, :], expd[s][:, :, DIM:2 * DIM], x2w[s][:, :, :],
                                       ALU.mult).then_inc(g2_xs, 1)
                    hold(pool, a2_full, t.lin(0, 1))
                    hold(pool, out_done[s], t.uses(-3, 16))
                    pool.tensor_tensor(y_sb[s][:, :, :], expd[s][:, :, 0:DIM], full_s[s][:, :, :], ALU.mult).then_inc(g2_sum, 1)
                    hold(pool, g2_sum, t.lin(-1, 4, 1))
                    pool.tensor_tensor(y_sb[s][:, :, :], y_sb[s][:, :, :], tiles_of(xr, t, -1), ALU.add).then_inc(g2_sum, 1)
                    hold(pool, g2_sum, t.lin(-1, 4, 2))
                    pool.tensor_tensor(y_sb[s][:, :, :], y_sb[s][:, :, :],
                                       bf_row[:, :].unsqueeze(1).broadcast_to([128, PAIRS, DIM]), ALU.add).then_inc(g2_sum, 1)
                    hold(pool, g2_sum, t.lin(-1, 4, 3))
                    hold(pool, a2_yin, t.lin(0, 1))
                    pool.tensor_tensor(y_sb[s][:, :, :], y_sb[s][:, :, :], yin[:, :, :], ALU.add).then_inc(g2_sum, 1)

            run2(pool, turn2)


_INPUTS = ("x", "ctxT", "wq", "wk", "wv", "wo", "bqk", "bv", "bo", "bf", "ffn_w", "conv", "gate_cols", "lin_w",
           "ident", "shift_rows", "v_frame")


def layouts(inp):
    f = np.float32
    p = {n.replace("L0_", ""): np.asarray(v) for n, v in inp.items()}

    def by_group(a):
        return a.reshape(GROUPS, 2, PAIRS, SEQ, DIM)

    order = np.arange(DIM).reshape(HEADS, DH).T.reshape(-1)
    conv = np.zeros((DIM, 2 * GATES), f)
    lin = np.zeros((2 * GATES + 1, 2 * DIM), f)
    for n, side in enumerate(("so", "si")):
        for g in range(GATES):
            conv[4 * g:4 * g + 4, n * GATES + g] = p[f"ffn_{side}_conv_w"][g]
        lin[n * GATES:(n + 1) * GATES, n * DIM:(n + 1) * DIM] = p[f"ffn_{side}_lin_w"].T
        lin[2 * GATES, n * DIM:(n + 1) * DIM] = p[f"ffn_{side}_lin_b"]
    shift = np.zeros((KROWS, HEADS, 2, HALF), mybir.dt.np(BF16))
    v_frame = np.zeros((2, SEQ, PAIRS, HEADS, 2, VW), f)
    for a in range(2):
        shift[MROWS + 2 * a:MROWS + 2 * a + 2, :, a, :] = -1.0
        v_frame[a, :, :, :, a, DH] = 1.0
    return {
        "x": by_group(p["x"]).transpose(1, 3, 0, 2, 4).reshape(128, TILES, DIM),
        "ctxT": by_group(p["ctx_1024"]).transpose(4, 0, 1, 3, 2).reshape(DIM, GROUPS, 2 * SEQ, PAIRS),
        "wq": p["xattn_Wq"].T[:, order], "wk": p["xattn_Wk"].T[:, order],
        "wv": p["xattn_Wv"].T, "wo": p["xattn_Wo"].T,
        "bqk": np.stack([p["xattn_bq"][order], p["xattn_bk"][order]], 1),
        "bv": np.repeat(p["xattn_bv"][:, None], 128, 1),
        "bo": np.repeat(p["xattn_bo"][None], 128, 0), "bf": np.repeat(p["ffn_bias"][None], 128, 0),
        "ffn_w": p["ffn_weight"], "conv": conv,
        "gate_cols": np.stack([np.concatenate([p[f"ffn_so_{n}"], p[f"ffn_si_{n}"]]) for n in ("conv_b", "gamma", "beta")], 1),
        "lin_w": lin, "ident": np.eye(128, dtype=f),
        "shift_rows": shift.reshape(KROWS, -1), "v_frame": v_frame.reshape(128, -1),
    }


def kernel(**inputs):
    import concourse.bacc as bacc
    from concourse.bass_utils import run_bass_kernel_spmd

    nc = bacc.Bacc("TRN2", target_bir_lowering=False, num_devices=1)
    arrays, args = {}, []
    for name, a in layouts(inputs).items():
        a = np.ascontiguousarray(a)
        arrays[f"in_{name}_dram"] = a
        args.append(nc.dram_tensor(f"in_{name}_dram", a.shape, mybir.dt.from_np(a.dtype), kind="ExternalInput").ap())
    args.append(nc.dram_tensor("out_dram", (128, TILES, DIM), F32, kind="ExternalOutput").ap())
    build(nc, *args)
    got = run_bass_kernel_spmd(nc, [arrays], core_ids=[0]).results[0]["out_dram"]
    return got.reshape(2, SEQ, GROUPS, PAIRS, DIM).transpose(2, 0, 3, 1, 4).reshape(BATCH, SEQ, DIM)
```

```python
from contextlib import ExitStack

import numpy as np

import concourse.bass as bass
from concourse import mybir

F32 = mybir.dt.float32
BF16 = mybir.dt.bfloat16
ALU = mybir.AluOpType
ACT = mybir.ActivationFunctionType
AX = mybir.AxisListType

BATCH, SEQ, DIM, HEADS = 128, 64, 128, 16
DH = DIM // HEADS
PAIRS = 4
GROUPS = BATCH // (2 * PAIRS)
TILES = GROUPS * PAIRS
GTOK = PAIRS * 2 * SEQ
HALF = PAIRS * SEQ
PARTS = 3
RUNS = (3, 2, 1)
ROWS = sum(RUNS) * DH
MROWS = 2 * ROWS
KROWS = MROWS + 4
VW = DH + 1
GATES = DIM // 4
TOPK = 32
LN_EPS = 1e-5
BN_EPS = 1e-5
SCALE = float(1.0 / np.sqrt(DH).astype(np.float32))
PICKED = -3.0e38
PT_RING = 4
SPLIT_DMAS = 2 * len(RUNS)


class Turn:

    def __init__(self, base, reg=None):
        self.base, self.reg = base, reg

    def lin(self, off, per, extra=0):
        if self.reg is None:
            return per * (self.base + off) + extra
        return self.reg * (2 * per) + (per * (self.base + off) + extra)

    def slot(self, off):
        return (self.base + off) % 2

    def uses(self, off, per, extra=0):
        if self.reg is None:
            return per * ((self.base + off) // 2 + 1) + extra
        return self.reg * per + (per * ((self.base + off) // 2 + 1) + extra)

    def has(self, off, groups=GROUPS):
        return self.reg is not None or 0 <= self.base + off < groups


def wait(eng, sem, value):
    if isinstance(value, int) and value <= 0:
        return
    eng.wait_ge(sem, value)


def build(nc, x, ctxT, wq, wk, wv, wo, bqk, bv, bo, bf, ffn_w, conv, gate_cols, lin_w, ident, shift_rows, v_frame, out):
    with ExitStack() as ctx:
        def sb(name, shape, dt=F32):
            return ctx.enter_context(nc.sbuf_tensor(name, shape, dt))

        def ps(name, shape, dt=F32):
            return ctx.enter_context(nc.psum_tensor(name, shape, dt))

        def sem(name):
            return ctx.enter_context(nc.semaphore(name))

        xr = sb("xr", [128, TILES, DIM])
        x2all = sb("x2all", [128, TILES, DIM])
        gates = sb("gates", [2 * GATES, TILES * 128])
        qst = [sb(f"qst{s}", [128, HEADS, HALF], BF16) for s in range(2)]
        kst = [sb(f"kst{s}", [128, HEADS, 2, SEQ * PAIRS], BF16) for s in range(2)]
        cT = [sb(f"cT{s}", [128, 2 * SEQ, PAIRS]) for s in range(2)]
        xn = [sb(f"xn{s}", [128, PAIRS, DIM]) for s in range(2)]
        xnT = sb("xnT", [128, 2, PAIRS, SEQ])
        q32 = sb("q32", [128, GTOK])
        k32 = sb("k32", [128, GTOK])
        q_rest = sb("q_rest", [128, GTOK])
        k_rest = sb("k_rest", [128, GTOK])
        q_parts = sb("q_parts", [128, PARTS, GTOK], BF16)
        k_parts = sb("k_parts", [128, PARTS, GTOK], BF16)
        vx = [sb(f"vx{s}", [128, PAIRS, HEADS, 2 * VW]) for s in range(2)]
        pT = sb("pT", [128, PT_RING, HEADS // 2, SEQ])
        attn = sb("attn", [128, 2, 2, DIM])
        attnT = sb("attnT", [128, 2, 2, 2 * SEQ])
        den = sb("den", [128, 2, HEADS, 2])
        x2w = [sb(f"x2w{s}", [128, PAIRS, DIM]) for s in range(2)]
        x2T = sb("x2T", [128, GTOK])
        m32 = sb("m32", [128, 2, 2, HEADS])
        m_parts = sb("m_parts", [128, 2, 2, 2, HEADS], BF16)
        mT = sb("mT", [64, 2, 128], BF16)
        st1 = sb("st1", [128, PAIRS, 6])
        st2 = sb("st2", [128, PAIRS, 6])
        ag1 = sb("ag1", [128, PAIRS, 2])
        ag2 = sb("ag2", [128, PAIRS, 2])
        ve1 = sb("ve1", [128, PAIRS])
        ve2 = sb("ve2", [128, PAIRS])
        rs1 = sb("rs1", [128, PAIRS])
        rs2 = sb("rs2", [128, PAIRS])
        nm1 = sb("nm1", [128, PAIRS])
        nm2 = sb("nm2", [128, PAIRS])
        gate_st = sb("gate_st", [2 * GATES, GROUPS, 6])
        gate_ag = sb("gate_ag", [2 * GATES, 2])
        gate_ab = sb("gate_ab", [2 * GATES, 4])
        idf = sb("idf", [128, 128])
        idb = sb("idb", [128, 128], BF16)
        wq_sb = sb("wq_sb", [128, DIM])
        wk_sb = sb("wk_sb", [128, DIM])
        wv_sb = sb("wv_sb", [128, DIM])
        wo_sb = sb("wo_sb", [128, DIM])
        wf_sb = sb("wf_sb", [128, DIM])
        conv_sb = sb("conv_sb", [128, 2 * GATES])
        lin_sb = sb("lin_sb", [2 * GATES + 1, 2 * DIM])
        bqk_sb = sb("bqk_sb", [128, 2])
        bv_wide = sb("bv_wide", [128, 128])
        bo_row = sb("bo_row", [128, DIM])
        bf_row = sb("bf_row", [128, DIM])
        gcol = sb("gcol", [2 * GATES, 3])
        half_neg = sb("half_neg", [128, PAIRS])
        picked, expd, gated_x, full_s, y_sb, g2 = [], [], [], [], [], []
        for s in range(2):
            room = kst[s][:, :, :, :].bitcast(F32).rearrange("p h a t -> p (h a t)")
            picked.append(room[:, 0:1024].rearrange("p (t c) -> p t c", t=PAIRS))
            expd.append(room[:, 1024:2048].rearrange("p (t c) -> p t c", t=PAIRS))
            gated_x.append(room[:, 2048:2560].rearrange("p (t c) -> p t c", t=PAIRS))
            full_s.append(room[:, 2560:3072].rearrange("p (t c) -> p t c", t=PAIRS))
            y_sb.append(room[:, 3072:3584].rearrange("p (t c) -> p t c", t=PAIRS))
            g2.append(room[:, 3584:4096])
        q_scratch = [nc.dram_tensor(f"q_scratch{s}", (128, PARTS, GTOK), BF16).ap() for s in range(2)]
        k_scratch = [nc.dram_tensor(f"k_scratch{s}", (128, PARTS, GTOK), BF16).ap() for s in range(2)]
        xsT = q32
        yin = k32[:, :].rearrange("q (p c) -> q p c", p=PAIRS)
        top_first = [sb(f"top_first{s}", [128, 2 * PAIRS, 8]) for s in range(2)]
        top_next = sb("top_next", [128, 2 * PAIRS, 8])
        neg_max = [sb(f"neg_max{s}", [128, 2 * PAIRS]) for s in range(2)]
        sums = [sb(f"sums{s}", [128, 2 * PAIRS]) for s in range(2)]
        rsum = [sb(f"rsum{s}", [128, 2 * PAIRS]) for s in range(2)]

        ps_turn = ps("ps_turn", [128, GTOK])
        ps_proj = ps("ps_proj", [128, GTOK])
        ps_row = [ps(f"ps_row{i}", [128, 4, 2, SEQ]) for i in range(2)]
        ps_col = [ps(f"ps_col{i}", [128, HEADS // 2, SEQ]) for i in range(2)]
        ps_pv = ps("ps_pv", [128, 512])
        ps_mix = ps("ps_mix", [128, 512])
        ps_logits = [[b[:, :, :, :].rearrange("q h a t -> q (h a t)").rearrange("q (t c) -> q t c", t=2) for b in ps_row],
                     [b[:, :, :].rearrange("q h t -> q (h t)").rearrange("q (t c) -> q t c", t=2) for b in ps_col]]
        pv_flat = [b[:, 0:HEADS * 2 * VW] for b in (ps_pv[:, :], ps_row[0][:, :, :, :].rearrange("q h a t -> q (h a t)"))]
        pv_view = [b.rearrange("q (h a v) -> q h a v", a=2, v=VW) for b in pv_flat]

        consts_in = sem("consts_in")
        x_in = [sem(f"x_in{s}") for s in range(2)]
        ctx_in = [sem(f"ctx_in{s}") for s in range(2)]
        q_moved = [sem(f"q_moved{s}") for s in range(2)]
        k_moved = [sem(f"k_moved{s}") for s in range(2)]
        q_out = [sem(f"q_out{s}") for s in range(2)]
        k_out = [sem(f"k_out{s}") for s in range(2)]
        m_moved = [[sem(f"m_moved{h}{s}") for s in range(2)] for h in range(2)]
        x2_kept = [sem(f"x2_kept{s}") for s in range(2)]
        pe_xT, pe_q, pe_k, pe_v = sem("pe_xT"), sem("pe_q"), sem("pe_k"), sem("pe_v")
        pe_row, pe_col, pe_pv = sem("pe_row"), sem("pe_col"), sem("pe_pv")
        pe_mT, pe_attnT, pe_out = sem("pe_mT"), sem("pe_attnT"), sem("pe_out")
        pe_x2T, pe_conv, pe_bias = sem("pe_x2T"), sem("pe_conv"), sem("pe_bias")
        act_ln1, act_xT, act_q, act_k, act_v = (sem(f"act_{n}") for n in ("ln1", "xT", "q", "k", "v"))
        act_mT, act_exp, act_attnT = sem("act_mT"), sem("act_exp"), sem("act_attnT")
        act_ln2, act_x2T, act_conv, act_gelu = (sem(f"act_{n}") for n in ("ln2", "x2T", "conv", "gelu"))
        dve_st1, dve_ag1, dve_st2, dve_ag2 = (sem(f"dve_{n}") for n in ("st1", "ag1", "st2", "ag2"))
        dve_max, dve_mhi, dve_m = sem("dve_max"), sem("dve_mhi"), sem("dve_m")
        dve_den, dve_attn, dve_x1, dve_gate = (sem(f"dve_{n}") for n in ("den", "attn", "x1", "gate"))
        dve_split = sem("dve_split")
        dve_bias, dve_setup = sem("dve_bias"), sem("dve_setup")
        gp_rs1, gp_rs2, gp_split, gp_xb, gp_bn = (sem(f"gp_{n}") for n in ("rs1", "rs2", "split", "xb", "bn"))
        g_in = [sem(f"g_in{s}") for s in range(2)]
        x2_in = [sem(f"x2_in{s}") for s in range(2)]
        p2_x2T, p2_lin, p2_full, p2_xsT, p2_yin = (sem(f"p2_{n}") for n in ("x2T", "lin", "full", "xsT", "yin"))
        a2_x2T, a2_exp, a2_left, a2_full, a2_xsT, a2_yin = (sem(f"a2_{n}") for n in ("x2T", "exp", "left", "full", "xsT", "yin"))
        d2_max, d2_rep, d2_rsum = sem("d2_max"), sem("d2_rep"), sem("d2_rsum")
        g2_neg, g2_gate, g2_xs, g2_sum = (sem(f"g2_{n}") for n in ("neg", "gate", "xs", "sum"))
        out_done = [sem(f"out_done{s}") for s in range(2)]
        passed = sem("passed")

        def hold(eng, semaphore, value):
            if isinstance(value, int):
                wait(eng, semaphore, value)
            else:
                eng.wait_ge(semaphore, value)
                eng.sem_inc(passed, 1)

        CONSTS = 13 + 2 * 2
        FIRST, LAST = -2, GROUPS + 1

        def run(eng, turn):
            for i in range(FIRST, 4):
                turn(Turn(i))
            with eng.Fori(0, (GROUPS - 8) // 2) as j:
                turn(Turn(4, j))
                turn(Turn(5, j))
            for i in range(GROUPS - 4, LAST + 1):
                turn(Turn(i))

        def run2(eng, turn):
            for i in range(-1, 3):
                turn(Turn(i))
            with eng.Fori(0, (GROUPS - 6) // 2) as j:
                turn(Turn(3, j))
                turn(Turn(4, j))
            for i in range(GROUPS - 3, GROUPS + 1):
                turn(Turn(i))

        def tiles_of(tensor, t, off):
            if t.reg is not None:
                return tensor[:, bass.ds(t.lin(off, PAIRS), PAIRS), :]
            g = t.base + off
            return tensor[:, PAIRS * g:PAIRS * (g + 1), :]

        def split(eng, whole, rest, parts, order, done, t):
            hold(eng, done, t.lin(1, 4))
            eng.tensor_copy(parts[:, order[0], :], whole[:, :]).then_inc(done, 1)
            hold(eng, done, t.lin(1, 4, 1))
            eng.tensor_tensor(rest[:, :], whole[:, :], parts[:, order[0], :], ALU.subtract).then_inc(done, 1)
            hold(eng, done, t.lin(1, 4, 2))
            eng.tensor_copy(parts[:, order[1], :], rest[:, :]).then_inc(done, 1)
            hold(eng, done, t.lin(1, 4, 3))
            eng.tensor_tensor(parts[:, order[2], :], rest[:, :], parts[:, order[1], :], ALU.subtract).then_inc(done, 1)

        block = ctx.enter_context(nc.Block())

        @block.sync
        def _(sp):
            for dst, src in ((idf, ident), (wq_sb, wq), (wk_sb, wk), (wv_sb, wv), (wo_sb, wo), (wf_sb, ffn_w),
                             (conv_sb, conv), (lin_sb, lin_w), (bqk_sb, bqk), (gcol, gate_cols),
                             (bv_wide, bv), (bo_row, bo), (bf_row, bf)):
                sp.dma_start(dst[:, :], src).then_inc(consts_in, 16)
            for s in range(2):
                sp.dma_start(xr[:, PAIRS * s:PAIRS * (s + 1), :], x[:, PAIRS * s:PAIRS * (s + 1), :]).then_inc(x_in[s], 16)
                sp.dma_start(cT[s][:, :, :], ctxT[:, s]).then_inc(ctx_in[s], 16)
            for s in range(2):
                sp.dma_start(vx[s][:, :, :, :].rearrange("k p h v -> k (p h v)"), v_frame).then_inc(consts_in, 16)
                sp.dma_start(kst[s][0:KROWS, :, :, :].rearrange("r h a t -> r (h a t)"), shift_rows).then_inc(consts_in, 16)

            def turn(t):
                if t.has(4):
                    hold(sp, dve_ag1, t.lin(3, 1))
                    sp.dma_start(tiles_of(xr, t, 4), tiles_of(x, t, 4)).then_inc(x_in[t.slot(4)], 16)
                if t.has(-2):
                    hold(sp, act_ln2, t.lin(-1, 1))
                    sp.dma_start(tiles_of(x2all, t, -2), x2w[t.slot(-2)][:, :, :]).then_inc(x2_kept[t.slot(-2)], 16)
                def max_rows(h):
                    hold(sp, act_mT, t.lin(0, 2, h + 1))
                    hold(sp, pe_col, t.lin(-1, 8))
                    sp.dma_start(qst[t.slot(0)][MROWS:KROWS, :, h * 128:(h + 1) * 128],
                                 mT[:, h, :]).then_inc(m_moved[h][t.slot(0)], 16)

                def stack(scratch, stacked, moved, a):
                    r = a * ROWS
                    for n in RUNS:
                        if stacked is qst:
                            dst, first = stacked[t.slot(1)][r:r + n * DH, :, :], 0
                        else:
                            dst, first = stacked[t.slot(1)][r:r + n * DH, :, a, :], PARTS - n
                        src = scratch[t.slot(1)][:, first:first + n, a * HALF:(a + 1) * HALF]
                        sp.dma_start(dst, src.rearrange("c n t -> n c t")).then_inc(moved[t.slot(1)], 16)
                        r += n * DH

                s = t.slot(1)
                if t.has(1):
                    hold(sp, gp_split, t.lin(2, 4))
                    hold(sp, k_moved[s], t.uses(-1, 16 * SPLIT_DMAS))
                    sp.dma_start(k_scratch[s], k_parts[:, :, :]).then_inc(k_out[s], 16)
                if t.has(0):
                    max_rows(0)
                if t.has(1):
                    hold(sp, pe_col, t.lin(0, 8))
                    hold(sp, k_out[s], t.uses(1, 16))
                    stack(k_scratch, kst, k_moved, 0)
                if t.has(0):
                    max_rows(1)
                if t.has(1):
                    stack(k_scratch, kst, k_moved, 1)
                    hold(sp, dve_split, t.lin(2, 4))
                    hold(sp, q_moved[s], t.uses(-1, 16 * SPLIT_DMAS))
                    sp.dma_start(q_scratch[s], q_parts[:, :, :]).then_inc(q_out[s], 16)
                    hold(sp, q_out[s], t.uses(1, 16))
                    stack(q_scratch, qst, q_moved, 0)
                    stack(q_scratch, qst, q_moved, 1)
                if t.has(3) and t.base + 3 >= 2:
                    hold(sp, pe_v, t.lin(2, 1))
                    sp.dma_start(cT[t.slot(3)][:, :, :], ctxT[:, bass.ds(t.lin(3, 1), 1)].rearrange("c g m p -> c (g m) p")
                                 if t.reg is not None else ctxT[:, t.base + 3]).then_inc(ctx_in[t.slot(3)], 16)

            run(sp, turn)

            def turn2(t):
                def gates_in(off):
                    s, g0 = t.slot(off), t.lin(off, GTOK)
                    hold(sp, act_gelu, t.lin(off + 1, 1))
                    sp.dma_start(g2[s][0:2 * GATES, :], gates[:, bass.ds(g0, GTOK)] if t.reg is not None
                                 else gates[:, g0:g0 + GTOK]).then_inc(g_in[s], 16)

                if t.base == -1:
                    sp.wait_ge(pe_col, 8 * GROUPS)
                    gates_in(1)
                if t.has(2) and t.base >= -1:
                    hold(sp, p2_lin, t.lin(1, 1))
                    gates_in(2)
                if t.has(1):
                    s = t.slot(1)
                    hold(sp, g2_xs, t.lin(0, 1))
                    hold(sp, p2_x2T, t.lin(0, 1))
                    sp.dma_start(x2w[s][:, :, :], tiles_of(x2all, t, 1)).then_inc(x2_in[s], 16)
                if t.has(-1):
                    s = t.slot(-1)
                    hold(sp, g2_sum, t.lin(-1, 4, 4))
                    sp.dma_start(tiles_of(out, t, -1), y_sb[s][:, :, :]).then_inc(out_done[s], 16)

            for s in range(2):
                sp.wait_ge(x2_kept[s], 16 * GROUPS // 2)
            run2(sp, turn2)
            for s in range(2):
                sp.wait_ge(out_done[s], 16 * GROUPS // 2)

        @block.tensor
        def _(pe):
            pe.wait_ge(consts_in, 16 * CONSTS)
            pe.wait_ge(dve_setup, 3)
            pe.matmul(ps_mix[:, 0:DIM], bv_wide[:, :], wo_sb[:, :], start=True, stop=True).then_inc(pe_bias, 1)

            def k_cols(s, rows, h, p):
                return kst[s][0:rows, h, :, :].rearrange("r a (m p) -> r (a m) p", p=PAIRS)[:, :, p]

            def key_side(t, p):
                s = t.slot(-1)
                if p % 2 == 0:
                    wait(pe, m_moved[p // 2][s], t.uses(-1, 16))
                for b in range(2):
                    wait(pe, act_exp, t.lin(-1, 8, 2 * p + b - 1))
                    for hh in range(HEADS // 2):
                        h = b * (HEADS // 2) + hh
                        mm = pe.matmul(ps_col[b][:, hh, :], k_cols(s, KROWS, h, p),
                                       qst[s][0:KROWS, h, p * SEQ:(p + 1) * SEQ], start=True, stop=True)
                    mm.then_inc(pe_col, 1)

            def values(t, p):
                s, pp = t.slot(-1), p % 2
                wait(pe, act_exp, t.lin(-1, 8, 2 * p + 2))
                if p == 0:
                    wait(pe, act_v, t.lin(0, 1))
                if p == 0:
                    wait(pe, dve_attn, t.lin(-1, 2, -1))
                if p == 2:
                    wait(pe, dve_max, t.lin(-1, 8, 7))
                for h in range(HEADS):
                    half = 2 * p + h // (HEADS // 2)
                    mm = pe.matmul(pv_flat[p // 2][pp * SEQ:(pp + 1) * SEQ, h * 2 * VW:(h + 1) * 2 * VW],
                                   pT[:, half % PT_RING, h % (HEADS // 2), :], vx[s][:, p, h, :], start=True, stop=True)
                mm.then_inc(pe_pv, 1)

            def turn_attn(t, hp):
                wait(pe, dve_attn, t.lin(-1, 2, hp + 1))
                wait(pe, dve_x1, t.lin(-1, 2, hp))
                if hp == 0:
                    wait(pe, act_mT, t.lin(0, 2))
                for a in range(2):
                    mm = pe.transpose(ps_mix[:, a * 128:(a + 1) * 128], attn[:, hp, a, :], idf[:, :])
                mm.then_inc(pe_attnT, 1)

            def out_proj(t, hp):
                wait(pe, act_attnT, t.lin(-1, 2, hp + 1))
                for pp in range(2):
                    mm = pe.matmul(ps_mix[:, pp * DIM:(pp + 1) * DIM], attnT[:, hp, pp, :], wo_sb[:, :],
                                   start=True, stop=True)
                mm.then_inc(pe_out, 1)

            def query_side(t, b):
                s, hp, j = t.slot(0), b // 4, b % 4
                if b == 0:
                    wait(pe, q_moved[s], t.uses(0, 16 * SPLIT_DMAS))
                    wait(pe, k_moved[s], t.uses(0, 16 * SPLIT_DMAS))
                    wait(pe, dve_attn, t.lin(-1, 2, 2))
                wait(pe, dve_max, t.lin(0, 8, b - 1))
                for hh in range(4):
                    h = 4 * j + hh
                    for pp in range(2):
                        p = 2 * hp + pp
                        mm = pe.matmul(ps_row[b % 2][pp * SEQ:(pp + 1) * SEQ, hh, :, :],
                                       qst[s][0:MROWS, h, p * SEQ:(p + 1) * SEQ],
                                       k_cols(s, MROWS, h, p), start=True, stop=True)
                mm.then_inc(pe_row, 1)

            def turn_max(t, hp):
                hold(pe, dve_m, t.lin(0, 2, hp + 1))
                hold(pe, dve_x1, t.lin(-1, 2, 2))
                hold(pe, act_mT, t.lin(0, 2, hp))
                pe.transpose(ps_mix[0:64, 0:64].bitcast(BF16), m_parts[:, hp, :, :, :].rearrange("q a x h -> q (a x h)"),
                             idb[:, :]).then_inc(pe_mT, 1)

            def turn(t):
                c, d, a, r = t.has(-1), t.has(-2), t.has(1), t.has(0)
                if c:
                    key_side(t, 0)
                    key_side(t, 1)
                    values(t, 0)
                    key_side(t, 2)
                    values(t, 1)
                    key_side(t, 3)
                    values(t, 2)
                    turn_attn(t, 0)
                    values(t, 3)
                if a:
                    wait(pe, ctx_in[t.slot(1)], t.uses(1, 16))
                    wait(pe, act_v, t.lin(1, 1))
                    pe.matmul(ps_proj[:, :], wk_sb[:, :], cT[t.slot(1)][:, :, :].rearrange("c m p -> c (m p)"),
                              start=True, stop=True).then_inc(pe_k, 1)
                if r:
                    query_side(t, 0)
                    query_side(t, 1)
                if c:
                    out_proj(t, 0)
                if a:
                    wait(pe, act_xT, t.lin(2, 1))
                    wait(pe, act_k, t.lin(2, 1))
                    pe.matmul(ps_proj[:, :], wq_sb[:, :], xnT[:, :, :, :].rearrange("c a p s -> c (a p s)"),
                              start=True, stop=True).then_inc(pe_q, 1)
                if r:
                    query_side(t, 2)
                    query_side(t, 3)
                if c:
                    turn_attn(t, 1)
                if d:
                    wait(pe, act_ln2, t.lin(-1, 1))
                    wait(pe, act_xT, t.lin(2, 1) if a else GROUPS)
                    for p in range(PAIRS):
                        mm = pe.transpose(ps_turn[:, p * 128:(p + 1) * 128], x2w[t.slot(-2)][:, p, :], idf[:, :])
                    mm.then_inc(pe_x2T, 1)
                if r:
                    query_side(t, 4)
                    query_side(t, 5)
                if c:
                    out_proj(t, 1)
                if r:
                    query_side(t, 6)
                    turn_max(t, 0)
                if d:
                    wait(pe, act_x2T, t.lin(-1, 1))
                    if a:
                        wait(pe, act_q, t.lin(2, 1))
                    else:
                        wait(pe, act_v, GROUPS)
                    wait(pe, act_conv, t.lin(-2, 1))
                    pe.matmul(ps_proj[0:2 * GATES, :], conv_sb[:, :], x2T[:, :], start=True, stop=True).then_inc(pe_conv, 1)
                if r:
                    query_side(t, 7)
                if t.has(2):
                    wait(pe, act_ln1, t.lin(3, 1))
                    wait(pe, act_x2T, t.lin(-1, 1))
                    wait(pe, act_xT, t.lin(2, 1))
                    for p in range(PAIRS):
                        mm = pe.transpose(ps_turn[:, p * 128:(p + 1) * 128], xn[t.slot(2)][:, p, :], idf[:, :])
                    mm.then_inc(pe_xT, 1)
                if a:
                    wait(pe, act_q, t.lin(2, 1))
                    wait(pe, act_conv, t.lin(-1, 1))
                    for p in range(PAIRS):
                        mm = pe.matmul(ps_proj[:, p * DIM:(p + 1) * DIM], cT[t.slot(1)][:, :, p], wv_sb[:, :],
                                       start=True, stop=True)
                    mm.then_inc(pe_v, 1)
                if r:
                    turn_max(t, 1)

            run(pe, turn)

            def turn2(t):
                if t.has(1):
                    s = t.slot(1)
                    wait(pe, g_in[s], t.uses(1, 16))
                    if t.base == -1:
                        wait(pe, gp_bn, 7)
                        wait(pe, dve_max, 8 * GROUPS)
                        wait(pe, act_exp, 8 * GROUPS)
                        wait(pe, dve_attn, 2 * GROUPS)
                    wait(pe, a2_exp, t.lin(0, 1))
                    wait(pe, d2_rep, t.lin(-1, 4, 1))
                    for p in range(PAIRS):
                        mm = pe.matmul(ps_logits[s][p // 2][:, p % 2, :], g2[s][0:2 * GATES + 1, p * 128:(p + 1) * 128],
                                       lin_sb[:, :], start=True, stop=True)
                    mm.then_inc(p2_lin, 1)
                if t.has(0):
                    s = t.slot(0)
                    wait(pe, x2_in[s], t.uses(0, 16))
                    wait(pe, a2_x2T, t.lin(0, 1))
                    for p in range(PAIRS):
                        mm = pe.transpose(ps_turn[:, p * 128:(p + 1) * 128], x2w[s][:, p, :], idf[:, :])
                    mm.then_inc(p2_x2T, 1)
                    wait(pe, a2_x2T, t.lin(1, 1))
                    wait(pe, a2_full, t.lin(0, 1))
                    for p in range(PAIRS):
                        mm = pe.matmul(ps_proj[:, p * DIM:(p + 1) * DIM], x2T[:, p * 128:(p + 1) * 128], wf_sb[:, :],
                                       start=True, stop=True)
                    mm.then_inc(p2_full, 1)
                if t.has(-1):
                    s = t.slot(-1)
                    wait(pe, g2_xs, t.lin(0, 1))
                    wait(pe, a2_xsT, t.lin(-1, 1))
                    for p in range(PAIRS):
                        mm = pe.transpose(ps_pv[:, p * 128:(p + 1) * 128], gated_x[s][:, p, :], idf[:, :])
                    mm.then_inc(p2_xsT, 1)
                    wait(pe, a2_xsT, t.lin(0, 1))
                    wait(pe, a2_yin, t.lin(-1, 1))
                    for p in range(PAIRS):
                        mm = pe.matmul(ps_mix[:, p * DIM:(p + 1) * DIM], xsT[:, p * 128:(p + 1) * 128], wf_sb[:, :],
                                       start=True, stop=True)
                    mm.then_inc(p2_yin, 1)

            run2(pe, turn2)

        @block.scalar
        def _(act):
            act.wait_ge(consts_in, 16 * CONSTS)

            def exp_half(t, b):
                wait(act, pe_col, t.lin(-1, 8, b + 1))
                wait(act, pe_pv, t.lin(-1, 4, (b - PT_RING) // 2 + 1))
                act.activation(pT[:, b % PT_RING, :, :], ps_col[b % 2][:, :, :], ACT.Exp, scale=SCALE).then_inc(act_exp, 1)

            def norm(t, off, src, dst, rs, nm):
                for p in range(PAIRS):
                    tile = src[:, bass.ds(t.lin(off, PAIRS, p), 1), :].rearrange("q o c -> q (o c)") if t.reg is not None \
                        else src[:, PAIRS * (t.base + off) + p, :]
                    ins = act.activation(dst[:, p, :], tile, ACT.Identity, bias=nm[:, p:p + 1], scale=rs[:, p:p + 1])
                return ins

            def attn_out(t, hp):
                wait(act, pe_attnT, t.lin(-1, 2, hp + 1))
                act.activation(attnT[:, hp, :, :].rearrange("d p (a s) -> d a p s", a=2),
                               ps_mix[:, 0:256].rearrange("d (a p s) -> d a p s", a=2, p=2), ACT.Copy).then_inc(act_attnT, 1)

            def max_out(t, hp):
                wait(act, pe_mT, t.lin(0, 2, hp + 1))
                wait(act, m_moved[hp][t.slot(-1)], t.uses(-1, 16))
                act.activation(mT[:, hp, :], ps_mix[0:64, 0:64].bitcast(BF16), ACT.Copy).then_inc(act_mT, 1)

            def turn(t):
                c, d, a, r = t.has(-1), t.has(-2), t.has(1), t.has(0)
                for b in range(8):
                    if c:
                        exp_half(t, b)
                    if b == 1 and r:
                        s = t.slot(0)
                        wait(act, pe_v, t.lin(1, 1))
                        wait(act, pe_pv, t.lin(-1, 4))
                        for half in range(2):
                            rows = slice(half * SEQ, (half + 1) * SEQ)
                            ins = act.activation(vx[s][rows, :, :, half * VW:half * VW + DH],
                                                 ps_proj[rows, :].rearrange("k (p h i) -> k p h i", p=PAIRS, i=DH), ACT.Copy)
                        ins.then_inc(act_v, 1)
                if c:
                    attn_out(t, 0)
                if d:
                    wait(act, gp_rs2, t.lin(-1, 4))
                    wait(act, x2_kept[t.slot(-4)], t.uses(-4, 16))
                    norm(t, -2, xr, x2w[t.slot(-2)], rs2, nm2).then_inc(act_ln2, 1)
                if t.has(2):
                    wait(act, gp_rs1, t.lin(3, 4))
                    wait(act, pe_xT, t.lin(1, 1))
                    norm(t, 2, xr, xn[t.slot(2)], rs1, nm1).then_inc(act_ln1, 1)
                if a:
                    wait(act, pe_k, t.lin(2, 1))
                    wait(act, gp_split, t.lin(1, 4))
                    act.activation(k32[:, :], ps_proj[:, :], ACT.Identity, bias=bqk_sb[:, 1:2]).then_inc(act_k, 1)
                if a:
                    wait(act, pe_q, t.lin(2, 1))
                    wait(act, dve_split, t.lin(1, 4))
                    act.activation(q32[:, :], ps_proj[:, :], ACT.Identity, bias=bqk_sb[:, 0:1]).then_inc(act_q, 1)
                if c:
                    attn_out(t, 1)
                if d:
                    wait(act, pe_x2T, t.lin(-1, 1))
                    wait(act, pe_conv, t.lin(-2, 1))
                    act.activation(x2T[:, :], ps_turn[:, :], ACT.Copy).then_inc(act_x2T, 1)
                if r:
                    max_out(t, 0)
                if d:
                    wait(act, pe_conv, t.lin(-1, 1))
                    g0 = t.lin(-2, GTOK)
                    act.activation(gates[:, bass.ds(g0, GTOK)] if t.reg is not None else gates[:, g0:g0 + GTOK],
                                   ps_proj[0:2 * GATES, :], ACT.Identity, bias=gcol[:, 0:1]).then_inc(act_conv, 1)
                if t.has(2):
                    wait(act, pe_xT, t.lin(3, 1))
                    wait(act, pe_q, t.lin(2, 1))
                    act.activation(xnT[:, :, :, :], ps_turn[:, :].rearrange("c (p a s) -> c a p s", a=2, s=SEQ),
                                   ACT.Copy).then_inc(act_xT, 1)
                if r:
                    max_out(t, 1)

            run(act, turn)

            act.wait_ge(act_conv, GROUPS)
            act.wait_ge(gp_bn, 5)
            for n in range(GROUPS):
                part = gates[:, n * GTOK:(n + 1) * GTOK]
                act.activation(part, part, ACT.Gelu, bias=gate_ab[:, 3:4], scale=gate_ab[:, 2:3]).then_inc(act_gelu, 1)

            def turn2(t):
                if t.has(-1):
                    s = t.slot(-1)
                    wait(act, d2_rep, t.lin(0, 4))
                    for p in range(PAIRS):
                        for gate in range(2):
                            tile = picked[s][:, p, gate * DIM:(gate + 1) * DIM]
                            n = 2 * p + gate
                            ins = act.activation(tile, tile, ACT.Exp, bias=neg_max[s][:, n:n + 1])
                    ins.then_inc(a2_left, 1)
                if t.has(0):
                    s = t.slot(0)
                    wait(act, p2_x2T, t.lin(1, 1))
                    wait(act, p2_full, t.lin(0, 1))
                    act.activation(x2T[:, :], ps_turn[:, :], ACT.Copy).then_inc(a2_x2T, 1)
                    wait(act, g2_neg, t.lin(1, 1))
                    wait(act, d2_rep, t.lin(0, 4, 1))
                    wait(act, g2_sum, t.lin(-1, 4))
                    wait(act, d2_rsum, t.lin(-1, 1))
                    for p in range(PAIRS):
                        for gate in range(2):
                            n = 2 * p + gate
                            ins = act.activation(expd[s][:, p, gate * DIM:(gate + 1) * DIM],
                                                 ps_logits[s][p // 2][:, p % 2, gate * DIM:(gate + 1) * DIM], ACT.Exp,
                                                 bias=neg_max[s][:, n:n + 1], accum_out=sums[s][:, n:n + 1])
                    ins.then_inc(a2_exp, 1)
                if t.has(-1):
                    s = t.slot(-1)
                    wait(act, p2_xsT, t.lin(0, 1))
                    wait(act, p2_yin, t.lin(-1, 1))
                    act.activation(xsT[:, :], ps_pv[:, :], ACT.Copy).then_inc(a2_xsT, 1)
                    wait(act, p2_yin, t.lin(0, 1))
                    wait(act, g2_sum, t.lin(-1, 4))
                    for p in range(PAIRS):
                        ins = act.activation(yin[:, p, :], ps_mix[:, p * DIM:(p + 1) * DIM], ACT.Copy,
                                             scale=rsum[s][:, 2 * p + 1:2 * p + 2])
                    ins.then_inc(a2_yin, 1)
                if t.has(0):
                    s = t.slot(0)
                    wait(act, p2_full, t.lin(1, 1))
                    wait(act, d2_rsum, t.lin(1, 1))
                    for p in range(PAIRS):
                        ins = act.activation(full_s[s][:, p, :], ps_proj[:, p * DIM:(p + 1) * DIM], ACT.Copy,
                                             scale=rsum[s][:, 2 * p:2 * p + 1])
                    ins.then_inc(a2_full, 1)

            run2(act, turn2)

        @block.vector
        def _(dve):
            dve.memset(half_neg[:, :], -0.5).then_inc(dve_setup, 1)
            dve.wait_ge(consts_in, 16 * CONSTS)
            dve.tensor_copy(idb[:, :], idf[:, :]).then_inc(dve_setup, 1)
            dve.memset(top_next[:, :, :], 0.0).then_inc(dve_setup, 1)
            dve.wait_ge(pe_bias, 1)
            dve.tensor_tensor(bo_row[:, :], bo_row[:, :], ps_mix[:, 0:DIM], ALU.add).then_inc(dve_bias, 1)

            def stats(t, off, st, ag, st_sem, ag_sem, used, used_count):
                hold(dve, ag_sem, t.lin(off, 1))
                for p in range(PAIRS):
                    tile = xr[:, bass.ds(t.lin(off, PAIRS, p), 1), :].rearrange("q o c -> q (o c)") if t.reg is not None \
                        else xr[:, PAIRS * (t.base + off) + p, :]
                    ins = dve.bn_stats(st[:, p, :], tile)
                ins.then_inc(st_sem, 1)
                hold(dve, used, used_count)
                hold(dve, st_sem, t.lin(off + 1, 1))
                for p in range(PAIRS):
                    ins = dve.bn_aggr(ag[:, p, :], st[:, p, :])
                ins.then_inc(ag_sem, 1)

            def normalise(t, hp):
                hold(dve, pe_pv, t.lin(-1, 4, 2 * hp + 2))
                hold(dve, dve_attn, t.lin(-2, 2, hp + 1))
                dve.reciprocal(den[:, hp, :, :], pv_view[hp][:, :, :, DH]).then_inc(dve_den, 1)
                hold(dve, pe_attnT, t.lin(-2, 2, hp + 1))
                hold(dve, dve_den, t.lin(-1, 2, hp + 1))
                for a in range(2):
                    ins = dve.tensor_tensor(attn[:, hp, a, :].rearrange("q (h i) -> q h i", i=DH), pv_view[hp][:, :, a, 0:DH],
                                            den[:, hp, :, a].unsqueeze(2).broadcast_to([128, HEADS, DH]), ALU.mult)
                ins.then_inc(dve_attn, 1)

            def residual(t, hp):
                hold(dve, pe_out, t.lin(-1, 2, hp + 1))
                hold(dve, gp_xb, t.lin(0, 1))
                tiles = xr[:, bass.ds(t.lin(-1, PAIRS, 2 * hp), 2), :] if t.reg is not None \
                    else xr[:, PAIRS * (t.base - 1) + 2 * hp:PAIRS * (t.base - 1) + 2 * hp + 2, :]
                dve.tensor_tensor(tiles, tiles, ps_mix[:, 0:2 * DIM].rearrange("q (p c) -> q p c", p=2),
                                  ALU.add).then_inc(dve_x1, 1)

            def row_max(t, b):
                hold(dve, pe_row, t.lin(0, 8, b + 1))
                j = b % 4
                if j == 0:
                    hold(dve, dve_m, t.lin(-1, 2, b // 4 + 1))
                dve.tensor_reduce(m32[:, b // 4, :, 4 * j:4 * j + 4].rearrange("q a h -> q h a"), ps_row[b % 2][:, :, :, :],
                                  AX.X, ALU.max).then_inc(dve_max, 1)

            def max_parts(t, hp):
                hold(dve, dve_max, t.lin(0, 8, 4 * hp + 4))
                hold(dve, pe_mT, t.lin(-1, 2, hp + 1))
                dve.tensor_copy(m_parts[:, hp, :, 0, :], m32[:, hp, :, :]).then_inc(dve_mhi, 1)
                hold(dve, dve_mhi, t.lin(0, 2, hp + 1))
                dve.tensor_tensor(m_parts[:, hp, :, 1, :], m32[:, hp, :, :], m_parts[:, hp, :, 0, :],
                                  ALU.subtract).then_inc(dve_m, 1)

            def turn(t):
                c, d, a, r = t.has(-1), t.has(-2), t.has(1), t.has(0)
                if c:
                    normalise(t, 0)
                if d:
                    hold(dve, dve_x1, t.lin(-1, 2))
                    stats(t, -2, st2, ag2, dve_st2, dve_ag2, gp_rs2, t.lin(-2, 4))
                if t.has(2):
                    hold(dve, x_in[t.slot(2)], t.uses(2, 16))
                    stats(t, 2, st1, ag1, dve_st1, dve_ag1, gp_rs1, t.lin(2, 4))
                if c:
                    normalise(t, 1)
                if r:
                    row_max(t, 0)
                    row_max(t, 1)
                if c:
                    residual(t, 0)
                if r:
                    row_max(t, 2)
                    row_max(t, 3)
                    max_parts(t, 0)
                    row_max(t, 4)
                    row_max(t, 5)
                if c:
                    residual(t, 1)
                if r:
                    row_max(t, 6)
                    row_max(t, 7)
                    max_parts(t, 1)
                if a:
                    hold(dve, act_q, t.lin(2, 1))
                    hold(dve, q_out[t.slot(0)], t.uses(0, 16))
                    split(dve, q32, q_rest, q_parts, (0, 1, 2), dve_split, t)
                if d:
                    hold(dve, act_conv, t.lin(-1, 1))
                    if t.reg is not None:
                        dve.bn_stats(gate_st[:, bass.ds(t.lin(-2, 1), 1), :].rearrange("c o n -> c (o n)"),
                                     gates[:, bass.ds(t.lin(-2, GTOK), GTOK)]).then_inc(dve_gate, 1)
                    else:
                        g = t.base - 2
                        dve.bn_stats(gate_st[:, g, :], gates[:, g * GTOK:(g + 1) * GTOK]).then_inc(dve_gate, 1)

            run(dve, turn)

            dve.wait_ge(dve_gate, GROUPS)
            dve.bn_aggr(gate_ag[:, :], gate_st[:, :, :].rearrange("c g n -> c (g n)")).then_inc(dve_gate, 1)

            def turn2(t):
                if t.has(0):
                    s = t.slot(0)
                    chains = [(2 * p + gate, p, gate) for p in range(PAIRS) for gate in range(2)]
                    hold(dve, p2_lin, t.lin(1, 1))
                    hold(dve, g2_gate, t.lin(-1, 1))
                    hold(dve, g2_neg, t.lin(-1, 1))
                    for rnd in range(TOPK // 8):
                        top = top_first[s] if rnd == 0 else top_next
                        if rnd:
                            hold(dve, d2_rep, t.lin(0, 4, rnd))
                        for n, p, gate in chains:
                            cols = slice(gate * DIM, (gate + 1) * DIM)
                            src = ps_logits[s][p // 2][:, p % 2, cols] if rnd == 0 else picked[s][:, p, cols]
                            ins = dve.max(top[:, n, :], src)
                        ins.then_inc(d2_max, 1)
                        hold(dve, d2_max, t.lin(0, 4, rnd + 1))
                        for n, p, gate in chains:
                            cols = slice(gate * DIM, (gate + 1) * DIM)
                            src = ps_logits[s][p // 2][:, p % 2, cols] if rnd == 0 else picked[s][:, p, cols]
                            ins = dve.match_replace(picked[s][:, p, cols], top[:, n, :], src, PICKED)
                        ins.then_inc(d2_rep, 1)
                        if rnd == 1:
                            hold(dve, a2_exp, t.lin(1, 1))
                            hold(dve, a2_yin, t.lin(-1, 1))
                            dve.reciprocal(rsum[s][:, :], sums[s][:, :]).then_inc(d2_rsum, 1)

            run2(dve, turn2)

        @block.gpsimd
        def _(pool):
            pool.wait_ge(dve_setup, 1)

            def rstd(t, off, ag, ve, rs, nm, ready, out_sem, used):
                hold(pool, out_sem, t.lin(off, 4))
                hold(pool, ready, t.lin(off + 1, 1))
                pool.tensor_scalar(ve[:, :], ag[:, :, 1], LN_EPS, None, ALU.add).then_inc(out_sem, 1)
                hold(pool, used, t.lin(off, 1))
                hold(pool, out_sem, t.lin(off, 4, 1))
                pool.tensor_tensor(rs[:, :], ve[:, :], half_neg[:, :], ALU.pow).then_inc(out_sem, 1)
                hold(pool, out_sem, t.lin(off, 4, 2))
                pool.tensor_tensor(nm[:, :], ag[:, :, 0], rs[:, :], ALU.mult).then_inc(out_sem, 1)
                hold(pool, out_sem, t.lin(off, 4, 3))
                pool.tensor_scalar(nm[:, :], nm[:, :], -1.0, None, ALU.mult).then_inc(out_sem, 1)

            def turn(t):
                if t.has(-2):
                    rstd(t, -2, ag2, ve2, rs2, nm2, dve_ag2, gp_rs2, act_ln2)
                if t.has(2):
                    rstd(t, 2, ag1, ve1, rs1, nm1, dve_ag1, gp_rs1, act_ln1)
                if t.has(1):
                    if t.base == -1 and t.reg is None:
                        pool.wait_ge(dve_bias, 1)
                    hold(pool, act_ln1, t.lin(2, 1))
                    tiles = tiles_of(xr, t, 1)
                    pool.tensor_tensor(tiles, tiles, bo_row[:, :].unsqueeze(1).broadcast_to([128, PAIRS, DIM]),
                                       ALU.add).then_inc(gp_xb, 1)
                    hold(pool, act_k, t.lin(2, 1))
                    hold(pool, k_out[t.slot(0)], t.uses(0, 16))
                    split(pool, k32, k_rest, k_parts, (2, 1, 0), gp_split, t)

            run(pool, turn)

            pool.wait_ge(dve_gate, GROUPS + 1)
            pool.tensor_scalar(gate_ab[:, 0:1], gate_ag[:, 1:2], BN_EPS, None, ALU.add).then_inc(gp_bn, 1)
            pool.wait_ge(gp_bn, 1)
            pool.tensor_tensor(gate_ab[:, 1:2], gate_ab[:, 0:1], half_neg[0:2 * GATES, 0:1], ALU.pow).then_inc(gp_bn, 1)
            pool.wait_ge(gp_bn, 2)
            pool.tensor_tensor(gate_ab[:, 2:3], gate_ab[:, 1:2], gcol[:, 1:2], ALU.mult).then_inc(gp_bn, 1)
            pool.wait_ge(gp_bn, 3)
            pool.tensor_tensor(gate_ab[:, 0:1], gate_ab[:, 2:3], gate_ag[:, 0:1], ALU.mult).then_inc(gp_bn, 1)
            pool.wait_ge(gp_bn, 4)
            pool.tensor_tensor(gate_ab[:, 3:4], gcol[:, 2:3], gate_ab[:, 0:1], ALU.subtract).then_inc(gp_bn, 1)
            pool.wait_ge(pe_col, 8 * GROUPS)
            for s in range(2):
                pool.memset(g2[s][2 * GATES:2 * GATES + 1, :], 1.0).then_inc(gp_bn, 1)

            def turn2(t):
                if t.has(0):
                    s = t.slot(0)
                    hold(pool, d2_max, t.lin(0, 4, 1))
                    hold(pool, a2_left, t.lin(-1, 1))
                    pool.tensor_scalar(neg_max[s][:, :], top_first[s][:, :, 0], -1.0, None, ALU.mult).then_inc(g2_neg, 1)
                if t.has(-1):
                    s = t.slot(-1)
                    hold(pool, a2_left, t.lin(0, 1))
                    pool.tensor_tensor(expd[s][:, :, :], expd[s][:, :, :], picked[s][:, :, :],
                                       ALU.subtract).then_inc(g2_gate, 1)
                    hold(pool, g2_gate, t.lin(0, 1))
                    pool.tensor_tensor(gated_x[s][:, :, :], expd[s][:, :, DIM:2 * DIM], x2w[s][:, :, :],
                                       ALU.mult).then_inc(g2_xs, 1)
                    hold(pool, a2_full, t.lin(0, 1))
                    hold(pool, out_done[s], t.uses(-3, 16))
                    pool.tensor_tensor(y_sb[s][:, :, :], expd[s][:, :, 0:DIM], full_s[s][:, :, :], ALU.mult).then_inc(g2_sum, 1)
                    hold(pool, g2_sum, t.lin(-1, 4, 1))
                    pool.tensor_tensor(y_sb[s][:, :, :], y_sb[s][:, :, :], tiles_of(xr, t, -1), ALU.add).then_inc(g2_sum, 1)
                    hold(pool, g2_sum, t.lin(-1, 4, 2))
                    pool.tensor_tensor(y_sb[s][:, :, :], y_sb[s][:, :, :],
                                       bf_row[:, :].unsqueeze(1).broadcast_to([128, PAIRS, DIM]), ALU.add).then_inc(g2_sum, 1)
                    hold(pool, g2_sum, t.lin(-1, 4, 3))
                    hold(pool, a2_yin, t.lin(0, 1))
                    pool.tensor_tensor(y_sb[s][:, :, :], y_sb[s][:, :, :], yin[:, :, :], ALU.add).then_inc(g2_sum, 1)

            run2(pool, turn2)


_INPUTS = ("x", "ctxT", "wq", "wk", "wv", "wo", "bqk", "bv", "bo", "bf", "ffn_w", "conv", "gate_cols", "lin_w",
           "ident", "shift_rows", "v_frame")


def layouts(inp):
    f = np.float32
    p = {n.replace("L0_", ""): np.asarray(v) for n, v in inp.items()}

    def by_group(a):
        return a.reshape(GROUPS, 2, PAIRS, SEQ, DIM)

    order = np.arange(DIM).reshape(HEADS, DH).T.reshape(-1)
    conv = np.zeros((DIM, 2 * GATES), f)
    lin = np.zeros((2 * GATES + 1, 2 * DIM), f)
    for n, side in enumerate(("so", "si")):
        for g in range(GATES):
            conv[4 * g:4 * g + 4, n * GATES + g] = p[f"ffn_{side}_conv_w"][g]
        lin[n * GATES:(n + 1) * GATES, n * DIM:(n + 1) * DIM] = p[f"ffn_{side}_lin_w"].T
        lin[2 * GATES, n * DIM:(n + 1) * DIM] = p[f"ffn_{side}_lin_b"]
    shift = np.zeros((KROWS, HEADS, 2, HALF), mybir.dt.np(BF16))
    v_frame = np.zeros((2, SEQ, PAIRS, HEADS, 2, VW), f)
    for a in range(2):
        shift[MROWS + 2 * a:MROWS + 2 * a + 2, :, a, :] = -1.0
        v_frame[a, :, :, :, a, DH] = 1.0
    return {
        "x": by_group(p["x"]).transpose(1, 3, 0, 2, 4).reshape(128, TILES, DIM),
        "ctxT": by_group(p["ctx_1024"]).transpose(4, 0, 1, 3, 2).reshape(DIM, GROUPS, 2 * SEQ, PAIRS),
        "wq": p["xattn_Wq"].T[:, order], "wk": p["xattn_Wk"].T[:, order],
        "wv": p["xattn_Wv"].T, "wo": p["xattn_Wo"].T,
        "bqk": np.stack([p["xattn_bq"][order], p["xattn_bk"][order]], 1),
        "bv": np.repeat(p["xattn_bv"][:, None], 128, 1),
        "bo": np.repeat(p["xattn_bo"][None], 128, 0), "bf": np.repeat(p["ffn_bias"][None], 128, 0),
        "ffn_w": p["ffn_weight"], "conv": conv,
        "gate_cols": np.stack([np.concatenate([p[f"ffn_so_{n}"], p[f"ffn_si_{n}"]]) for n in ("conv_b", "gamma", "beta")], 1),
        "lin_w": lin, "ident": np.eye(128, dtype=f),
        "shift_rows": shift.reshape(KROWS, -1), "v_frame": v_frame.reshape(128, -1),
    }


def kernel(**inputs):
    import concourse.bacc as bacc
    from concourse.bass_utils import run_bass_kernel_spmd

    nc = bacc.Bacc("TRN2", target_bir_lowering=False, num_devices=1)
    arrays, args = {}, []
    for name, a in layouts(inputs).items():
        a = np.ascontiguousarray(a)
        arrays[f"in_{name}_dram"] = a
        args.append(nc.dram_tensor(f"in_{name}_dram", a.shape, mybir.dt.from_np(a.dtype), kind="ExternalInput").ap())
    args.append(nc.dram_tensor("out_dram", (128, TILES, DIM), F32, kind="ExternalOutput").ap())
    build(nc, *args)
    got = run_bass_kernel_spmd(nc, [arrays], core_ids=[0]).results[0]["out_dram"]
    return got.reshape(2, SEQ, GROUPS, PAIRS, DIM).transpose(2, 0, 3, 1, 4).reshape(BATCH, SEQ, DIM)
```
